# Optimizing a Trainium2 kernel written in Bass

```python
import numpy as np
import jax
import jax.numpy as jnp

def _softmax(x, axis=-1):
    return jax.nn.softmax(x, axis=axis)

def _gelu(x):
    return jax.nn.gelu(x, approximate=True)

def _silu(x):
    return jax.nn.silu(x)

def _sigmoid(x):
    return jax.nn.sigmoid(x)

def _layernorm(x, axis=-1, eps=1e-05):
    m = jnp.mean(x, axis=axis, keepdims=True)
    v = jnp.var(x, axis=axis, keepdims=True)
    return (x - m) / jnp.sqrt(v + eps)

def _scatter_add(tgt, idx, src, axis=0):
    return tgt.at[idx].add(src)

def _segment_sum(src, seg, n):
    return jax.ops.segment_sum(src, seg, n)
kernel_name = 'mk_xattn_seq_d1_seqx_r4_2725b1'

def setup_inputs(seed: int=0):
    np.random.seed(seed)
    _w = jnp.asarray

    def _rec_inputs():
        import jax
        import jax.numpy as jnp
        _rk = jax.random.key(seed)
        x = -0.0002928 + 1 * jax.random.normal(jax.random.fold_in(_rk, 1), (32, 256, 256), jnp.float32)
        _lenS = 256 - jax.random.randint(jax.random.fold_in(_rk, 7), (32,), 0, max(1, 256 // 4) + 1, jnp.int32)
        _lenS2 = 256 - jax.random.randint(jax.random.fold_in(_rk, 8), (32,), 0, max(1, 256 // 4) + 1, jnp.int32)
        _ctx_1024P = jax.random.normal(jax.random.fold_in(_rk, 11), (32, 16, 256), jnp.float32)
        _ctx_1024c = jax.random.dirichlet(jax.random.fold_in(_rk, 511), 0.3 * jnp.ones((16,), jnp.float32), (32, 256))
        _ctx_1024t = jnp.einsum('bsk,bkd->bsd', _ctx_1024c, _ctx_1024P)
        _ctx_1024t = _ctx_1024t * jax.lax.rsqrt(jnp.mean(jnp.square(_ctx_1024t)) + 1e-12) * 0.953939
        ctx_1024 = -1.39393e-06 + 0.999914 * (_ctx_1024t + 0.3 * jax.random.normal(jax.random.fold_in(_rk, 611), (32, 256, 256), jnp.float32))
        return (x, ctx_1024)
    x, ctx_1024 = _rec_inputs()

    def _L0_xattn_setup():
        import jax, jax.numpy as jnp
        import numpy as np
        D_MODEL = 256
        N_HEADS = 16
        D_K = D_MODEL // N_HEADS
        LN_EPS = 1e-05

        def _attention(query, key_value, W_qkv, b_qkv, W_o, b_o, ln_gamma, ln_beta):
            B, Sq, _ = query.shape
            Skv = key_value.shape[1]
            Wq, Wk, Wv = (W_qkv[:D_MODEL], W_qkv[D_MODEL:2 * D_MODEL], W_qkv[2 * D_MODEL:])
            bq, bk, bv = (b_qkv[:D_MODEL], b_qkv[D_MODEL:2 * D_MODEL], b_qkv[2 * D_MODEL:])
            Q = (query @ Wq.T + bq).reshape(B, Sq, N_HEADS, D_K).transpose(0, 2, 1, 3)
            K = (key_value @ Wk.T + bk).reshape(B, Skv, N_HEADS, D_K).transpose(0, 2, 1, 3)
            V = (key_value @ Wv.T + bv).reshape(B, Skv, N_HEADS, D_K).transpose(0, 2, 1, 3)
            scores = jnp.einsum('bhqd,bhkd->bhqk', Q.astype(jnp.float32), K.astype(jnp.float32))
            scores = scores / np.sqrt(D_K)
            attn = jax.nn.softmax(scores, axis=-1)
            context = jnp.einsum('bhqk,bhkd->bhqd', attn, V.astype(jnp.float32)).astype(query.dtype)
            context = context.transpose(0, 2, 1, 3).reshape(B, Sq, D_MODEL)
            output = context @ W_o.T + b_o
            x = output + query
            mu = jnp.mean(x, axis=-1, keepdims=True)
            var = jnp.mean(jnp.square(x - mu), axis=-1, keepdims=True)
            return (x - mu) / jnp.sqrt(var + LN_EPS) * ln_gamma + ln_beta
        key = jax.random.key(seed)
        ks = jax.random.split(key, 8)
        B, Sq, Skv = (2, 512, 512)
        scale = 1.0 / np.sqrt(D_MODEL)
        return {'query': jax.random.normal(ks[0], (B, Sq, D_MODEL), dtype=jnp.float32), 'key_value': jax.random.normal(ks[1], (B, Skv, D_MODEL), dtype=jnp.float32), 'W_qkv': jax.random.normal(ks[2], (3 * D_MODEL, D_MODEL), dtype=jnp.float32) * scale, 'b_qkv': jax.random.normal(ks[3], (3 * D_MODEL,), dtype=jnp.float32) * 0.01, 'W_o': jax.random.normal(ks[4], (D_MODEL, D_MODEL), dtype=jnp.float32) * scale, 'b_o': jax.random.normal(ks[5], (D_MODEL,), dtype=jnp.float32) * 0.01, 'ln_gamma': jnp.ones((D_MODEL,), dtype=jnp.float32), 'ln_beta': jnp.zeros((D_MODEL,), dtype=jnp.float32)}
    _L0_xattn_all = _L0_xattn_setup()
    _L0_xattn_in = {k: v for k, v in _L0_xattn_all.items() if k in ('W_qkv', 'b_qkv', 'W_o', 'b_o', 'ln_gamma', 'ln_beta')}
    del _L0_xattn_all
    return {'x': x, 'ctx_1024': ctx_1024, 'L0_xattn_W_qkv': _L0_xattn_in['W_qkv'], 'L0_xattn_b_qkv': _L0_xattn_in['b_qkv'], 'L0_xattn_W_o': _L0_xattn_in['W_o'], 'L0_xattn_b_o': _L0_xattn_in['b_o'], 'L0_xattn_ln_gamma': _L0_xattn_in['ln_gamma'], 'L0_xattn_ln_beta': _L0_xattn_in['ln_beta']}

def reference(x, ctx_1024, L0_xattn_W_qkv, L0_xattn_b_qkv, L0_xattn_W_o, L0_xattn_b_o, L0_xattn_ln_gamma, L0_xattn_ln_beta):
    import jax
    import jax.numpy as jnp

    def _L0_xattn_ref(query, key_value, W_qkv, b_qkv, W_o, b_o, ln_gamma, ln_beta):
        import jax, jax.numpy as jnp
        import numpy as np
        D_MODEL = 256
        N_HEADS = 16
        D_K = D_MODEL // N_HEADS
        LN_EPS = 1e-05

        def _attention(query, key_value, W_qkv, b_qkv, W_o, b_o, ln_gamma, ln_beta):
            B, Sq, _ = query.shape
            Skv = key_value.shape[1]
            Wq, Wk, Wv = (W_qkv[:D_MODEL], W_qkv[D_MODEL:2 * D_MODEL], W_qkv[2 * D_MODEL:])
            bq, bk, bv = (b_qkv[:D_MODEL], b_qkv[D_MODEL:2 * D_MODEL], b_qkv[2 * D_MODEL:])
            Q = (query @ Wq.T + bq).reshape(B, Sq, N_HEADS, D_K).transpose(0, 2, 1, 3)
            K = (key_value @ Wk.T + bk).reshape(B, Skv, N_HEADS, D_K).transpose(0, 2, 1, 3)
            V = (key_value @ Wv.T + bv).reshape(B, Skv, N_HEADS, D_K).transpose(0, 2, 1, 3)
            scores = jnp.einsum('bhqd,bhkd->bhqk', Q.astype(jnp.float32), K.astype(jnp.float32))
            scores = scores / np.sqrt(D_K)
            attn = jax.nn.softmax(scores, axis=-1)
            context = jnp.einsum('bhqk,bhkd->bhqd', attn, V.astype(jnp.float32)).astype(query.dtype)
            context = context.transpose(0, 2, 1, 3).reshape(B, Sq, D_MODEL)
            output = context @ W_o.T + b_o
            x = output + query
            mu = jnp.mean(x, axis=-1, keepdims=True)
            var = jnp.mean(jnp.square(x - mu), axis=-1, keepdims=True)
            return (x - mu) / jnp.sqrt(var + LN_EPS) * ln_gamma + ln_beta
        return _attention(query, key_value, W_qkv, b_qkv, W_o, b_o, ln_gamma, ln_beta)
    x = _L0_xattn_ref(x, ctx_1024, L0_xattn_W_qkv, L0_xattn_b_qkv, L0_xattn_W_o, L0_xattn_b_o, L0_xattn_ln_gamma, L0_xattn_ln_beta)
    return x

_drawn_inputs = setup_inputs


def setup_inputs(seed=0):
    import zlib

    import numpy as np

    out = dict(_drawn_inputs(seed))
    spreads = {'L0_xattn_ln_gamma': (1.0, 0.2), 'L0_xattn_ln_beta': (0.0, 0.1)}
    factors = {'L0_xattn_b_qkv': 6.5, 'L0_xattn_b_o': 6.237}
    for name, (base, spread) in spreads.items():
        noise = np.random.default_rng([zlib.crc32(name.encode()), seed]).standard_normal(out[name].shape)
        drawn = base * np.exp(spread * noise) if base else spread * noise
        out[name] = jnp.asarray(drawn.astype(out[name].dtype))
    for name, factor in factors.items():
        out[name] = (out[name] * factor).astype(out[name].dtype)
    return out
```

```python
from contextlib import ExitStack

import concourse.bass as bass
from concourse import mybir

F32 = mybir.dt.float32
F32R = mybir.dt.float32r
ALU = mybir.AluOpType
ACT = mybir.ActivationFunctionType
AX = mybir.AxisListType

P = 128
B = 32
S = 256
D = 256
H = 16
DK = D // H
KT = D // P
GROUPS = 4
GH = H // GROUPS
PAIRS = H // 2
MP = PAIRS // KT
HALF = 64
PARTS = 3 * DK
ROWS = PARTS + 2
EPS = 1e-5
SCALE = 1.0 / DK ** 0.5

BANKS = 3
SHARED = [
    (0, 0, "qk0", 1), (0, 1, "max_turn1", -1), (0, 2, "stack", 0, 6), (0, 3, "stack", 0, 7),
    (1, 0, "qk1", 1), (1, 1, "stack", 1, 0), (1, 2, "out_turn", -2, 0), (1, 2, "out_turn", -2, 1), (1, 3, "stack", 1, 1),
    (2, 0, "v", 0), (2, 1, "max_turn0", 0), (2, 1, "ctx_turn", -2), (2, 2, "stack", 1, 2), (2, 3, "stack", 1, 3),
    (3, 0, "out_proj", -2), (3, 1, "stack", 1, 4), (3, 3, "stack", 1, 5), (3, 3, "nothing", 0),
]
FIRST_SLOT, LAST_SLOT = -1, B + 2
LOOP_FROM, LOOP_TO = 4, B - 4


def live(batch):
    return not isinstance(batch, int) or 0 <= batch < B


def uses_at(g, i):
    return [(k, use) for k, use in enumerate(SHARED) if use[0] == g and use[1] == i]


def last_use(n, k):
    slot, k = n, k - BANKS
    while True:
        if k < 0:
            slot, k = slot - 1, k + len(SHARED)
        if isinstance(slot, int) and slot < FIRST_SLOT:
            return None
        if SHARED[k][2] != "nothing" and live(slot + SHARED[k][3]):
            return slot, SHARED[k]
        k -= BANKS


def wait(eng, sem, value):
    if not isinstance(value, int) or value > 0:
        eng.wait_ge(sem, value)


def slots(eng, slot):
    for n in range(FIRST_SLOT, LOOP_FROM):
        slot(n, n % 2)
    with eng.Fori(LOOP_FROM, LOOP_TO, 2) as n:
        slot(n, 0)
        slot(n + 1, 1)
    for n in range(LOOP_TO, LAST_SLOT + 1):
        slot(n, n % 2)


def xattn_kernel(nc, x_t, c_t, x, w, b_q_k, b_v, rows, select, ident_in, ones_rows_in, out):
    with ExitStack() as ctx:
        def sb(name, shape, dt=F32):
            return ctx.enter_context(nc.sbuf_tensor(name, shape, dt))

        def sem(name):
            return ctx.enter_context(nc.semaphore(name))

        w_raw = sb("w_raw", [P, KT, 4, D])
        w_hi = sb("w_hi", [P, KT, 4, D], F32R)
        w_lo = sb("w_lo", [P, KT, 4, D], F32R)
        sel_raw = sb("sel_raw", [P, 4, MP, P])
        sel = sb("sel", [P, 4, MP, P], F32R)
        bias_qk = sb("bias_qk", [P, 2 * KT])
        bias_v = sb("bias_v", [P, KT])
        bias_v_wide = sb("bias_v_wide", [P, KT, P])
        row_params = sb("row_params", [P, 3, D])
        bias_out = sb("bias_out", [P, D])
        ident = sb("ident", [P, P])
        ones_rows = sb("ones_rows", [P, 1])
        xc_raw = [sb(f"xc_raw{p}", [P, 2, KT, S]) for p in range(2)]
        xc_hi = [sb(f"xc_hi{p}", [P, 2, KT, S], F32R) for p in range(2)]
        xc_lo = [sb(f"xc_lo{p}", [P, 2, KT, S], F32R) for p in range(2)]
        qk_raw = [sb(f"qk_raw{m}", [P, 2, S]) for m in range(KT)]
        qk_hi = [sb(f"qk_hi{m}", [P, 2, S], F32R) for m in range(KT)]
        qk_lo = [sb(f"qk_lo{m}", [P, 2, S], F32R) for m in range(KT)]
        stack = [sb(f"stack{p}", [P, PAIRS, 2, S], F32R) for p in range(2)]
        v_ones = [sb(f"v_ones{p}", [P, KT, H, 2 * DK]) for p in range(2)]
        row_max = sb("row_max", [P, KT, 2, PAIRS])
        neg_max = [sb(f"neg_max{m}", [P, KT, 2, 2, MP]) for m in range(2)]
        neg_max_t = [sb(f"neg_max_t{m}", [4 * MP, S], F32R) for m in range(2)]
        probs = sb("probs", [P, 2 * GH, KT, S])
        ctx_t = [sb(f"ctx_t{p}", [P, GROUPS, S]) for p in range(2)]
        inv_sum = sb("inv_sum", [P, KT, H])
        context = sb("context", [P, KT, D])
        context_hi = sb("context_hi", [P, KT, S], F32R)
        context_lo = sb("context_lo", [P, KT, S], F32R)
        x_in = [sb(f"x_in{p}", [P, KT, D]) for p in range(2)]
        z = [sb(f"z{p}", [P, KT, D]) for p in range(2)]
        stats = sb("stats", [P, KT, 6])
        mean_var = [sb(f"mean_var{p}", [P, KT, 2]) for p in range(2)]
        log_var = sb("log_var", [P, KT])
        rstd = sb("rstd", [P, KT])
        eps_col = sb("eps_col", [P, 1])
        one_col = sb("one_col", [P, 1])
        normed = [sb(f"normed{p}", [P, KT, D]) for p in range(2)]
        max_dram = [nc.dram_tensor(f"max_dram{m}", [2, 2, MP * S], F32).ap() for m in range(2)]

        shared = [ctx.enter_context(nc.psum_tensor(f"shared{k}", [P, 512], F32)) for k in range(BANKS)]
        max_ps = [ctx.enter_context(nc.psum_tensor(f"max_ps{k}", [P, KT, S], F32)) for k in range(2)]
        score_ps = [ctx.enter_context(nc.psum_tensor(f"score_ps{k}", [P, KT, S], F32)) for k in range(2)]
        ctx_ps = ctx.enter_context(nc.psum_tensor("ctx_ps", [P, 512], F32))

        weights_in, consts_in, rows_in = sem("weights_in"), sem("consts_in"), sem("rows_in")
        weights_split, consts_done, ones_set = sem("weights_split"), sem("consts_done"), sem("ones_set")
        bias_prod, bias_out_done = sem("bias_prod"), sem("bias_out_done")
        xc_in = [sem(f"xc_in{p}") for p in range(2)]
        x_in_loaded = [sem(f"x_in_loaded{p}") for p in range(2)]
        xc_hi_done, xc_lo_done = sem("xc_hi_done"), sem("xc_lo_done")
        qk_full, qk_raw_done = sem("qk_full"), sem("qk_raw_done")
        stack_full, stack_done = sem("stack_full"), sem("stack_done")
        v_full, v_done = sem("v_full"), sem("v_done")
        max_t_full = [sem(f"max_t_full{m}") for m in range(2)]
        max_t_done = [sem(f"max_t_done{m}") for m in range(2)]
        out_turn_full, context_done = sem("out_turn_full"), sem("context_done")
        ctx_turn_full, context_lo_done = sem("ctx_turn_full"), sem("context_lo_done")
        out_full, z_done = sem("out_full"), sem("z_done")
        qk_hi_done, qk_lo_done = sem("qk_hi_done"), sem("qk_lo_done")
        max_full, max_done = sem("max_full"), sem("max_done")
        neg_hi_done, neg_lo_done = sem("neg_hi_done"), sem("neg_lo_done")
        max_out = [sem(f"max_out{m}") for m in range(2)]
        max_rows_in = [sem(f"max_rows_in{m}") for m in range(2)]
        score_full, exp_done = sem("score_full"), sem("exp_done")
        ctx_full, ctx_taken = sem("ctx_full"), sem("ctx_taken")
        inv_done, context_hi_done = sem("inv_done"), sem("context_hi_done")
        x_bias_done = sem("x_bias_done")
        stats_done, mean_var_done = sem("stats_done"), sem("mean_var_done")
        log_done, rstd_done = sem("log_done"), sem("rstd_done")
        norm_done, gamma_done, beta_done = sem("norm_done"), sem("gamma_done"), sem("beta_done")
        stored = [sem(f"stored{p}") for p in range(2)]

        block = ctx.enter_context(nc.Block())

        @block.sync
        def _(sp):
            def load_xc(b, par):
                wait(sp, xc_lo_done, 2 * (b - 1))
                sp.dma_start(xc_raw[par][:, 0], x_t[b].rearrange("(k p) s -> p k s", p=P)).then_inc(xc_in[par], 16)
                sp.dma_start(xc_raw[par][:, 1], c_t[b].rearrange("(k p) s -> p k s", p=P)).then_inc(xc_in[par], 16)

            def max_rows(b, par, half):
                wait(sp, max_t_done[half], b + 1)
                sp.dma_start(max_dram[half].rearrange("e a (j s) -> (e a j) s", s=S),
                             neg_max_t[half][:, :].bitcast(F32)).then_inc(max_out[half], 16)
                sp.wait_ge(max_out[half], 16 * (b + 1))
                for side in range(2):
                    row = HALF * side + PARTS
                    sp.dma_start(stack[par][row:row + 2, MP * half:MP * (half + 1), 0, :].bitcast(F32),
                                 max_dram[half][side].rearrange("a (j s) -> a j s", s=S)
                                 ).then_inc(max_rows_in[half], 16)

            def slot(n, par):
                if live(n - 1):
                    max_rows(n - 1, 1 - par, 1)
                if live(n + 3):
                    load_xc(n + 3, 1 - par)
                if live(n - 1):
                    wait(sp, z_done, n - 2)
                    sp.dma_start(x_in[1 - par][:, :, :], x[n - 1].rearrange("(t p) d -> p t d", p=P)
                                 ).then_inc(x_in_loaded[1 - par], 16)
                if live(n - 3):
                    wait(sp, beta_done, n - 2)
                    sp.dma_start(out[n - 3].rearrange("(t p) d -> p t d", p=P), normed[1 - par][:, :, :]
                                 ).then_inc(stored[1 - par], 16)
                if live(n):
                    max_rows(n, par, 0)

            sp.dma_start(w_raw[:, :, :, :], w.rearrange("(k p) a d -> p k a d", p=P)).then_inc(weights_in, 16)
            load_xc(0, 0)
            sp.dma_start(sel_raw[:, :, :, :], select).then_inc(consts_in, 16)
            sp.dma_start(bias_qk[:, :], b_q_k).then_inc(consts_in, 16)
            sp.dma_start(ones_rows[:, :], ones_rows_in).then_inc(consts_in, 16)
            load_xc(1, 1)
            sp.dma_start(bias_v[:, :], b_v).then_inc(rows_in, 16)
            sp.dma_start(row_params[:, :, :], rows.unsqueeze(0).broadcast_to([P, 3, D])).then_inc(rows_in, 16)
            sp.dma_start(ident[:, :], ident_in).then_inc(rows_in, 16)
            slots(sp, slot)
            for p in range(2):
                sp.wait_ge(stored[p], 16 * B // 2)

        @block.tensor
        def _(pe):
            def three_passes(dst, stationary, moving):
                terms = [(a, c, k) for k in range(KT) for a, c in ((0, 0), (1, 0), (0, 1))]
                for t, (a, c, k) in enumerate(terms):
                    mm = nc.tensor.matmul(dst, stationary[a](k), moving[c](k), start=t == 0, stop=t == len(terms) - 1)
                return mm

            def bank_read(n, k):
                last = last_use(n, k)
                if last is None:
                    return
                b, what = last[0] + last[1][3], last[1][2]
                if what in ("qk0", "qk1"):
                    pe.wait_ge(qk_raw_done, 2 * b + int(what[2]) + 1)
                elif what == "stack":
                    pe.wait_ge(stack_done, PAIRS * b + last[1][4] + 1)
                elif what == "v":
                    pe.wait_ge(v_done, b + 1)
                elif what in ("max_turn0", "max_turn1"):
                    pe.wait_ge(max_t_done[int(what[8])], b + 1)
                elif what == "out_turn":
                    pe.wait_ge(context_done, KT * b + last[1][4] + 1)
                elif what == "ctx_turn":
                    pe.wait_ge(context_lo_done, b + 1)
                else:
                    pe.wait_ge(z_done, b + 1)

            def shared_work(k, use, n, par):
                b, what = n + use[3], use[2]
                if what == "nothing" or not live(b):
                    return
                bp = (par + use[3]) % 2
                ps = shared[k % BANKS]
                if what in ("qk0", "qk1"):
                    m = int(what[2])
                    pe.wait_ge(xc_lo_done, 2 * (b + 1))
                    bank_read(n, k)
                    for a in range(2):
                        mm = three_passes(ps[:, a * S:(a + 1) * S],
                                          [lambda kt, a=a, t=t: t[:, kt, a, m * P:(m + 1) * P] for t in (w_hi, w_lo)],
                                          [lambda kt, a=a, t=t: t[bp][:, a, kt, :] for t in (xc_hi, xc_lo)])
                    mm.then_inc(qk_full, 1)
                elif what == "stack":
                    pair = use[4]
                    m, j = divmod(pair, MP)
                    pe.wait_ge(qk_lo_done, 2 * b + m + 1)
                    bank_read(n, k)
                    for a in range(2):
                        nc.tensor.matmul(ps[:, a * S:(a + 1) * S], sel[:, 2 * a, j, :], qk_hi[m][:, a, :],
                                         start=True, stop=False)
                        mm = nc.tensor.matmul(ps[:, a * S:(a + 1) * S], sel[:, 2 * a + 1, j, :], qk_lo[m][:, a, :],
                                              start=False, stop=True)
                    mm.then_inc(stack_full, 1)
                elif what == "v":
                    bank_read(n, k)
                    for t in range(KT):
                        mm = three_passes(ps[:, t * D:(t + 1) * D],
                                          [lambda kt, t=t, u=u: u[bp][:, 1, kt, t * P:(t + 1) * P] for u in (xc_hi, xc_lo)],
                                          [lambda kt, u=u: u[:, kt, 2, :] for u in (w_hi, w_lo)])
                    mm.then_inc(v_full, 1)
                elif what in ("max_turn0", "max_turn1"):
                    half = int(what[8])
                    pe.wait_ge(neg_lo_done, 2 * b + half + 1)
                    bank_read(n, k)
                    for t in range(KT):
                        mm = nc.tensor.transpose(ps[0:4 * MP, t * P:(t + 1) * P],
                                                 neg_max[half][:, t].rearrange("p e a j -> p (e a j)"), ident[:, :])
                    mm.then_inc(max_t_full[half], 1)
                elif what == "out_turn":
                    t = use[4]
                    pe.wait_ge(ctx_taken, GROUPS * (b + 1))
                    bank_read(n, k)
                    for g in range(GROUPS):
                        mm = nc.tensor.transpose(ps[:, g * P:(g + 1) * P], ctx_t[bp][:, g, t * P:(t + 1) * P], ident[:, :])
                    mm.then_inc(out_turn_full, 1)
                elif what == "ctx_turn":
                    pe.wait_ge(context_done, KT * (b + 1))
                    bank_read(n, k)
                    for k2 in range(KT):
                        for t in range(KT):
                            mm = nc.tensor.transpose(ps[:, k2 * S + t * P:k2 * S + (t + 1) * P],
                                                     context[:, t, k2 * P:(k2 + 1) * P], ident[:, :])
                    mm.then_inc(ctx_turn_full, 1)
                else:
                    pe.wait_ge(context_lo_done, b + 1)
                    bank_read(n, k)
                    for t in range(KT):
                        mm = three_passes(ps[:, t * D:(t + 1) * D],
                                          [lambda kt, t=t, u=u: u[:, kt, t * P:(t + 1) * P] for u in (context_hi, context_lo)],
                                          [lambda kt, u=u: u[:, kt, 3, :] for u in (w_hi, w_lo)])
                    mm.then_inc(out_full, 1)

            def slot(n, par):
                for g in range(GROUPS):
                    for i in range(GH):
                        c, pair, base = GH * g + i, 2 * g + i // 2, HALF * (i % 2)
                        if live(n):
                            if i % 2 == 0:
                                pe.wait_ge(stack_done, PAIRS * n + pair + 1)
                            wait(pe, max_done, H * n + c - 1)
                            for t in range(KT):
                                mm = nc.tensor.matmul(max_ps[c % 2][:, t, :],
                                                      stack[par][base:base + PARTS, pair, 0, t * P:(t + 1) * P],
                                                      stack[par][base:base + PARTS, pair, 1, :], start=True, stop=True)
                            mm.then_inc(max_full, 1)
                        if live(n - 1):
                            if g % 2 == 0 and i == 0:
                                pe.wait_ge(max_rows_in[g // 2], 32 * n)
                            wait(pe, exp_done, H * (n - 1) + c - 1)
                            for t in range(KT):
                                mm = nc.tensor.matmul(score_ps[c % 2][:, t, :],
                                                      stack[1 - par][base:base + ROWS, pair, 1, t * P:(t + 1) * P],
                                                      stack[1 - par][base:base + ROWS, pair, 0, :], start=True, stop=True)
                            mm.then_inc(score_full, 1)
                        if i == 1:
                            b, vg, bp = (n - 2, GROUPS - 1, par) if g == 0 else (n - 1, g - 1, 1 - par)
                            if live(b):
                                group = GROUPS * b + vg
                                pe.wait_ge(exp_done, GH * (group + 1))
                                pe.wait_ge(v_done, b + 1)
                                wait(pe, ctx_taken, group)
                                for t in range(KT):
                                    for j in range(GH):
                                        mm = nc.tensor.matmul(ctx_ps[32 * j:32 * j + 32, 0:S],
                                                              v_ones[bp][:, t, GH * vg + j, :],
                                                              probs[:, GH * (vg % 2) + j, t, :],
                                                              start=t == 0, stop=t == KT - 1)
                                mm.then_inc(ctx_full, 1)
                        for k, use in uses_at(g, i):
                            shared_work(k, use, n, par)

            pe.wait_ge(weights_split, 2)
            pe.wait_ge(consts_done, 2)
            for kt in range(KT):
                mm = nc.tensor.matmul(ctx_ps[:, 0:D], bias_v_wide[:, kt, :], w_raw[:, kt, 3, :],
                                      start=kt == 0, stop=kt == KT - 1)
            mm.then_inc(bias_prod, 1)
            slots(pe, slot)

        @block.scalar
        def _(act):
            def shared_read(k, use, n, par):
                b, what = n + use[3], use[2]
                if not live(b) or what in ("out_turn", "out_proj", "nothing"):
                    return
                bp = (par + use[3]) % 2
                ps = shared[k % BANKS]
                if what in ("qk0", "qk1"):
                    m = int(what[2])
                    act.wait_ge(qk_full, 2 * b + m + 1)
                    wait(act, qk_lo_done, 2 * b + m - 1)
                    nc.scalar.activation(qk_raw[m][:, 0, :], ps[:, 0:S], ACT.Identity, bias=bias_qk[:, 2 * m:2 * m + 1])
                    nc.scalar.activation(qk_raw[m][:, 1, :], ps[:, S:2 * S], ACT.Identity,
                                         bias=bias_qk[:, 2 * m + 1:2 * m + 2]).then_inc(qk_raw_done, 1)
                elif what == "stack":
                    act.wait_ge(stack_full, PAIRS * b + use[4] + 1)
                    nc.scalar.activation(stack[bp][:, use[4], :, :].rearrange("p a s -> p (a s)"), ps[:, :], ACT.Identity,
                                         bias=ones_rows[:, 0:1]).then_inc(stack_done, 1)
                elif what == "v":
                    act.wait_ge(v_full, b + 1)
                    nc.scalar.copy(v_ones[bp][:, :, :, 0:DK].rearrange("p t h d -> p (t h) d"),
                                   ps[:, :].rearrange("p (h d) -> p h d", d=DK)).then_inc(v_done, 1)
                elif what in ("max_turn0", "max_turn1"):
                    half = int(what[8])
                    act.wait_ge(max_t_full[half], b + 1)
                    wait(act, max_out[half], 16 * b)
                    nc.scalar.copy(neg_max_t[half][:, :], ps[0:4 * MP, 0:S]).then_inc(max_t_done[half], 1)
                else:
                    act.wait_ge(ctx_turn_full, b + 1)
                    nc.scalar.copy(context_hi[:, :, :].rearrange("p k s -> p (k s)"), ps[:, :]).then_inc(context_hi_done, 1)

            def slot(n, par):
                for g in range(GROUPS):
                    for i in range(GH):
                        c = GH * g + i
                        if live(n - 1):
                            act.wait_ge(score_full, H * (n - 1) + c + 1)
                            nc.scalar.activation(probs[:, GH * (g % 2) + i, :, :], score_ps[c % 2][:, :, :], ACT.Exp,
                                                 scale=SCALE).then_inc(exp_done, 1)
                        for k, use in uses_at(g, i):
                            shared_read(k, use, n, par)
                        if i == 2:
                            b, vg, bp = (n - 2, GROUPS - 1, par) if g == 0 else (n - 1, g - 1, 1 - par)
                            if live(b):
                                act.wait_ge(ctx_full, GROUPS * b + vg + 1)
                                nc.scalar.copy(ctx_t[bp][:, vg, :], ctx_ps[:, 0:S]).then_inc(ctx_taken, 1)
                        if (g, i) == (0, 1) and live(n - 3):
                            act.wait_ge(mean_var_done, KT * (n - 2))
                            wait(act, norm_done, KT * (n - 3))
                            nc.scalar.activation(log_var[:, :], mean_var[1 - par][:, :, 1], ACT.Ln,
                                                 bias=eps_col[:, 0:1]).then_inc(log_done, 1)
                            act.wait_ge(log_done, n - 2)
                            nc.scalar.activation(rstd[:, :], log_var[:, :], ACT.Exp, scale=-0.5).then_inc(rstd_done, 1)

            nc.scalar.preload_act_table_set("natural_log_exp_and_others")
            act.wait_ge(consts_in, 48)
            act.wait_ge(ones_set, 3)
            slots(act, slot)

        @block.vector
        def _(dve):
            def negate(n, half):
                hi, lo = neg_max[half][:, :, :, 0, :], neg_max[half][:, :, :, 1, :]
                top = row_max[:, :, :, MP * half:MP * (half + 1)]
                dve.wait_ge(max_done, H * n + H // 2 * (half + 1))
                nc.vector.tensor_scalar(hi.bitcast(F32R), top, -1.0, None, ALU.mult).then_inc(neg_hi_done, 1)
                dve.wait_ge(neg_hi_done, 2 * n + half + 1)
                nc.vector.scalar_tensor_tensor(out=lo, in0=top, scalar=-1.0, in1=hi, op0=ALU.mult,
                                               op1=ALU.subtract).then_inc(neg_lo_done, 1)

            def divide(b, bank_of):
                for t in range(KT):
                    dve.wait_ge(out_turn_full, KT * b + t + 1)
                    heads = shared[bank_of[t]][:, :].rearrange("p (h c) -> p h c", c=2 * DK)
                    nc.vector.reciprocal(inv_sum[:, t, :], heads[:, :, DK]).then_inc(inv_done, 1)
                for t in range(KT):
                    heads = shared[bank_of[t]][:, :].rearrange("p (h c) -> p h c", c=2 * DK)
                    dve.wait_ge(inv_done, KT * b + t + 1)
                    nc.vector.tensor_tensor(context[:, t, :].rearrange("p (h d) -> p h d", d=DK), heads[:, :, 0:DK],
                                            inv_sum[:, t, :].unsqueeze(2).broadcast_to([P, H, DK]),
                                            ALU.mult).then_inc(context_done, 1)

            banks = {use[2:]: k % BANKS for k, use in enumerate(SHARED)}

            def slot(n, par):
                for g in range(GROUPS):
                    for i in range(GH):
                        c = GH * g + i
                        if (g, i) == (3, 2) and live(n - 2):
                            dve.wait_ge(stats_done, KT * (n - 1))
                        if live(n):
                            dve.wait_ge(max_full, H * n + c + 1)
                            nc.vector.tensor_reduce(row_max[:, :, i % 2, 2 * g + i // 2], max_ps[c % 2][:, :, :], AX.X,
                                                    ALU.max).then_inc(max_done, 1)
                            if (g, i) in ((1, 3), (3, 3)):
                                negate(n, g // 2)
                        b = n - 2
                        if not live(b):
                            continue
                        if (g, i) == (1, 3):
                            divide(b, [banks["out_turn", -2, t] for t in range(KT)])
                        elif (g, i) == (2, 2):
                            dve.wait_ge(context_hi_done, b + 1)
                            nc.vector.tensor_tensor(context_lo[:, :, :].rearrange("p k s -> p (k s)"),
                                                    shared[banks["ctx_turn", -2]][:, :],
                                                    context_hi[:, :, :].rearrange("p k s -> p (k s)"),
                                                    ALU.subtract).then_inc(context_lo_done, 1)
                        elif (g, i) == (3, 1):
                            dve.wait_ge(out_full, b + 1)
                            dve.wait_ge(x_bias_done, b + 1)
                            wait(dve, norm_done, KT * (b - 1))
                            nc.vector.tensor_tensor(z[par][:, :, :].rearrange("p t d -> p (t d)"),
                                                    shared[banks["out_proj", -2]][:, :],
                                                    x_in[par][:, :, :].rearrange("p t d -> p (t d)"),
                                                    ALU.add).then_inc(z_done, 1)
                            dve.wait_ge(z_done, b + 1)
                            for t in range(KT):
                                nc.vector.bn_stats(stats[:, t, :], z[par][:, t, :]).then_inc(stats_done, 1)
                        elif (g, i) == (3, 2):
                            for t in range(KT):
                                nc.vector.bn_aggr(mean_var[par][:, t, :], stats[:, t, :]).then_inc(mean_var_done, 1)

            dve.wait_ge(weights_in, 16)
            nc.vector.tensor_copy(w_hi[:, :, :, :], w_raw[:, :, :, :]).then_inc(weights_split, 1)
            dve.wait_ge(weights_split, 1)
            nc.vector.tensor_tensor(w_lo[:, :, :, :], w_raw[:, :, :, :], w_hi[:, :, :, :],
                                    ALU.subtract).then_inc(weights_split, 1)
            dve.wait_ge(consts_in, 48)
            nc.vector.tensor_copy(sel[:, :, :, :], sel_raw[:, :, :, :]).then_inc(consts_done, 1)
            dve.wait_ge(rows_in, 48)
            nc.vector.tensor_copy(bias_v_wide[:, :, :], bias_v[:, :].unsqueeze(2).broadcast_to([P, KT, P])
                                  ).then_inc(consts_done, 1)
            dve.wait_ge(bias_prod, 1)
            nc.vector.tensor_tensor(bias_out[:, :], ctx_ps[:, 0:D], row_params[:, 0, :],
                                    ALU.add).then_inc(bias_out_done, 1)
            slots(dve, slot)

        @block.gpsimd
        def _(pool):
            def split_xc(b, bp, a):
                wait(pool, xc_in[bp], 16 * (b - bp) + 32)
                if a == 1:
                    wait(pool, v_full, b - 1)
                nc.gpsimd.tensor_tensor(xc_hi[bp][:, a], xc_raw[bp][:, a],
                                        one_col[:, :].unsqueeze(2).broadcast_to([P, KT, S]),
                                        ALU.mult).then_inc(xc_hi_done, 1)
                pool.wait_ge(xc_hi_done, 2 * b + a + 1)
                nc.gpsimd.tensor_tensor(xc_lo[bp][:, a], xc_raw[bp][:, a], xc_hi[bp][:, a],
                                        ALU.subtract).then_inc(xc_lo_done, 1)

            def split_qk(b, m):
                wait(pool, qk_raw_done, 2 * b + m + 1)
                nc.gpsimd.tensor_tensor(qk_hi[m][:, :, :], qk_raw[m][:, :, :],
                                        one_col[:, :].unsqueeze(2).broadcast_to([P, 2, S]),
                                        ALU.mult).then_inc(qk_hi_done, 1)
                pool.wait_ge(qk_hi_done, 2 * b + m + 1)
                nc.gpsimd.tensor_tensor(qk_lo[m][:, :, :], qk_raw[m][:, :, :], qk_hi[m][:, :, :],
                                        ALU.subtract).then_inc(qk_lo_done, 1)

            def slot(n, par):
                if live(n + 1):
                    split_qk(n + 1, 0)
                if live(n - 2):
                    pool.wait_ge(x_in_loaded[par], 8 * (n - 2 - par) + 16)
                    nc.gpsimd.tensor_tensor(x_in[par][:, :, :], x_in[par][:, :, :],
                                            bias_out[:, :].unsqueeze(1).broadcast_to([P, KT, D]),
                                            ALU.add).then_inc(x_bias_done, 1)
                if live(n + 2):
                    split_xc(n + 2, par, 0)
                if live(n - 3):
                    pool.wait_ge(rstd_done, n - 2)
                    wait(pool, stored[1 - par], 8 * (n - 3 - (1 - par)))
                if live(n + 1):
                    split_qk(n + 1, 1)
                if live(n - 3):
                    b, bp = n - 3, 1 - par
                    for t in range(KT):
                        nc.gpsimd.tensor_scalar(normed[bp][:, t, :], z[bp][:, t, :], mean_var[bp][:, t, 0:1],
                                                rstd[:, t:t + 1], ALU.subtract, ALU.mult).then_inc(norm_done, 1)
                    pool.wait_ge(norm_done, KT * (b + 1))
                    nc.gpsimd.tensor_tensor(normed[bp][:, :, :], normed[bp][:, :, :],
                                            row_params[:, 1, :].unsqueeze(1).broadcast_to([P, KT, D]),
                                            ALU.mult).then_inc(gamma_done, 1)
                    pool.wait_ge(gamma_done, b + 1)
                    nc.gpsimd.tensor_tensor(normed[bp][:, :, :], normed[bp][:, :, :],
                                            row_params[:, 2, :].unsqueeze(1).broadcast_to([P, KT, D]),
                                            ALU.add).then_inc(beta_done, 1)
                if live(n + 2):
                    split_xc(n + 2, par, 1)

            for p in range(2):
                nc.gpsimd.memset(v_ones[p][:, :, :, :], 1.0).then_inc(ones_set, 1)
            nc.gpsimd.memset(eps_col[:, :], EPS).then_inc(ones_set, 1)
            nc.gpsimd.memset(one_col[:, :], 1.0).then_inc(ones_set, 1)
            pool.wait_ge(ones_set, 4)
            for a in range(2):
                split_xc(0, 0, a)
            pool.wait_ge(bias_out_done, 1)
            slots(pool, slot)


def kernel(x, ctx_1024, L0_xattn_W_qkv, L0_xattn_b_qkv, L0_xattn_W_o, L0_xattn_b_o, L0_xattn_ln_gamma, L0_xattn_ln_beta):
    import numpy as np
    from concourse import bacc
    from concourse.bass_utils import run_bass_kernel_spmd

    x, c = np.asarray(x), np.asarray(ctx_1024)
    w_qkv, w_o = np.asarray(L0_xattn_W_qkv), np.asarray(L0_xattn_W_o)
    b_qkv = np.asarray(L0_xattn_b_qkv)

    order = np.arange(D).reshape(KT, MP, 2, DK).transpose(0, 2, 1, 3).reshape(D)
    w = np.stack([w_qkv[:D][order].T, w_qkv[D:2 * D][order].T, w_qkv[2 * D:].T, w_o.T], axis=1)
    b_q_k = np.stack([b_qkv[a * D:(a + 1) * D][order][m * P:(m + 1) * P] for m in range(KT) for a in range(2)], axis=1)

    select = np.zeros((P, 4, MP, P), np.float32)
    for kind, places in enumerate(((0, 2), (1,), (0, 1), (2,))):
        for side in range(2):
            for j in range(MP):
                for place in places:
                    for d in range(DK):
                        select[HALF * side + DK * j + d, kind, j, HALF * side + DK * place + d] = 1
    ones_rows = np.zeros((P, 1), np.float32)
    for side in range(2):
        ones_rows[HALF * side + PARTS:HALF * side + ROWS] = 1

    arrays = {
        "x_t": x.transpose(0, 2, 1), "c_t": c.transpose(0, 2, 1), "x": x, "w": w, "b_q_k": b_q_k, "b_v": b_qkv[2 * D:].reshape(KT, P).T,
        "rows": np.stack([np.asarray(L0_xattn_b_o), np.asarray(L0_xattn_ln_gamma), np.asarray(L0_xattn_ln_beta)]),
        "select": select, "ident": np.eye(P, dtype=np.float32), "ones_rows": ones_rows,
    }
    arrays = {f"in_{name}": np.ascontiguousarray(a) for name, a in arrays.items()}
    nc = bacc.Bacc("TRN2", target_bir_lowering=False, num_devices=1)
    args = [nc.dram_tensor(name, a.shape, mybir.dt.from_np(a.dtype), kind="ExternalInput").ap() for name, a in arrays.items()]
    args.append(nc.dram_tensor("out", (B, S, D), F32, kind="ExternalOutput").ap())
    xattn_kernel(nc, *args)
    return run_bass_kernel_spmd(nc, [arrays], core_ids=[0]).results[0]["out"]
```

```python
from contextlib import ExitStack

import concourse.bass as bass
from concourse import mybir

F32 = mybir.dt.float32
F32R = mybir.dt.float32r
ALU = mybir.AluOpType
ACT = mybir.ActivationFunctionType
AX = mybir.AxisListType

P = 128
B = 32
S = 256
D = 256
H = 16
DK = D // H
KT = D // P
GROUPS = 4
GH = H // GROUPS
PAIRS = H // 2
MP = PAIRS // KT
HALF = 64
PARTS = 3 * DK
ROWS = PARTS + 2
EPS = 1e-5
SCALE = 1.0 / DK ** 0.5

BANKS = 3
SHARED = [
    (0, 0, "qk0", 1, 0, 0), (0, 0, "max_turn1", -1, 1, 0), (0, 1, "stack", 0, 2, 5), (0, 2, "qk0", 1, 0, 1),
    (0, 3, "stack", 0, 1, 6),
    (1, 0, "qk1", 1, 2, 0), (1, 0, "out_turn", -2, 0, 0), (1, 1, "stack", 0, 1, 7), (1, 2, "qk1", 1, 2, 1),
    (1, 2, "out_turn", -2, 0, 1), (1, 3, "stack", 1, 1, 0),
    (2, 0, "v", 0, 0, 0), (2, 0, "max_turn0", 0, 2, 0), (2, 0, "ctx_turn", -2, 1, 0), (2, 1, "stack", 1, 2, 1),
    (2, 2, "v", 0, 0, 1), (2, 3, "stack", 1, 2, 2),
    (3, 0, "out_proj", -2, 1, 0), (3, 1, "stack", 1, 0, 3), (3, 2, "out_proj", -2, 1, 1), (3, 3, "stack", 1, 2, 4),
]
PROJECTIONS = ("qk0", "qk1", "v", "out_proj")
FIRST_SLOT, LAST_SLOT = -1, B + 2
LOOP_FROM, LOOP_TO = 4, B - 4


def live(batch):
    return not isinstance(batch, int) or 0 <= batch < B


def is_last(batch):
    return isinstance(batch, int) and batch == B - 1


def uses_at(g, i):
    return [(k, use) for k, use in enumerate(SHARED) if use[0] == g and use[1] == i]


def last_use(n, k):
    slot, bank = n, SHARED[k][4]
    while True:
        k -= 1
        if k < 0:
            slot, k = slot - 1, len(SHARED) - 1
        if isinstance(slot, int) and slot < FIRST_SLOT:
            return None
        if SHARED[k][4] == bank and live(slot + SHARED[k][3]):
            return slot, SHARED[k]


def wait(eng, sem, value):
    if not isinstance(value, int) or value > 0:
        eng.wait_ge(sem, value)


def slots(eng, slot, after_first=None):
    slot(FIRST_SLOT, FIRST_SLOT % 2)
    if after_first:
        after_first()
    for n in range(FIRST_SLOT + 1, LOOP_FROM):
        slot(n, n % 2)
    with eng.Fori(LOOP_FROM, LOOP_TO, 2) as n:
        slot(n, 0)
        slot(n + 1, 1)
    for n in range(LOOP_TO, LAST_SLOT + 1):
        slot(n, n % 2)


def xattn_kernel(nc, x_t, c_t, x, w, b_q_k, b_v, rows, select, ident_in, ones_rows_in, out):
    with ExitStack() as ctx:
        def sb(name, shape, dt=F32):
            return ctx.enter_context(nc.sbuf_tensor(name, shape, dt))

        def sem(name):
            return ctx.enter_context(nc.semaphore(name))

        w_raw = sb("w_raw", [P, KT, 4, D])
        w_hi = sb("w_hi", [P, KT, 4, D], F32R)
        w_lo = sb("w_lo", [P, KT, 4, D], F32R)
        sel_raw = sb("sel_raw", [P, 2, 2, 2, P])
        sel = sb("sel", [P, 2, 2, 2, P], F32R)
        bias_qk = sb("bias_qk", [P, 2 * KT])
        bias_v = sb("bias_v", [P, KT])
        bias_v_wide = sb("bias_v_wide", [P, KT, P])
        row_params = sb("row_params", [P, 3, D])
        bias_out = sb("bias_out", [P, D])
        ident = sb("ident", [P, P])
        ones_rows = sb("ones_rows", [P, 1])
        xc_raw = [sb(f"xc_raw{p}", [P, 2, KT, S]) for p in range(2)]
        xc_hi = [sb(f"xc_hi{p}", [P, 2, KT, S], F32R) for p in range(2)]
        xc_lo = [sb(f"xc_lo{p}", [P, 2, KT, S], F32R) for p in range(2)]
        qk_raw = [sb(f"qk_raw{m}", [P, 2, S]) for m in range(KT)]
        qk_parts = [[sb(f"qk_parts{m}{f}", [P, 2, S], F32R) for f in range(2)] for m in range(KT)]
        stack = [sb(f"stack{p}", [P, PAIRS, 2, S], F32R) for p in range(2)]
        v_ones = [sb(f"v_ones{p}", [P, KT, H, 2 * DK]) for p in range(2)]
        row_max = sb("row_max", [P, KT, 2, PAIRS])
        neg_max = [sb(f"neg_max{m}", [P, KT, 2, 2, MP]) for m in range(2)]
        neg_max_t = [sb(f"neg_max_t{m}", [4 * MP, S], F32R) for m in range(2)]
        probs = sb("probs", [P, 2 * GH, KT, S])
        ctx_t = [sb(f"ctx_t{p}", [P, GROUPS, S]) for p in range(2)]
        inv_sum = sb("inv_sum", [P, KT, H])
        context = sb("context", [P, KT, D])
        context_hi = sb("context_hi", [P, KT, S], F32R)
        context_lo = sb("context_lo", [P, KT, S], F32R)
        x_in = [sb(f"x_in{p}", [P, KT, D]) for p in range(2)]
        z = [sb(f"z{p}", [P, KT, D]) for p in range(2)]
        stats = sb("stats", [P, KT, 6])
        mean_var = [sb(f"mean_var{p}", [P, KT, 2]) for p in range(2)]
        log_var = sb("log_var", [P, KT])
        rstd = sb("rstd", [P, KT])
        eps_col = sb("eps_col", [P, 1])
        one_col = sb("one_col", [P, 1])
        normed = [sb(f"normed{p}", [P, KT, D]) for p in range(2)]
        shared = [ctx.enter_context(nc.psum_tensor(f"shared{k}", [P, 512], F32)) for k in range(BANKS)]
        max_ps = [ctx.enter_context(nc.psum_tensor(f"max_ps{k}", [P, KT, S], F32)) for k in range(2)]
        score_ps = [ctx.enter_context(nc.psum_tensor(f"score_ps{k}", [P, KT, S], F32)) for k in range(2)]
        ctx_ps = ctx.enter_context(nc.psum_tensor("ctx_ps", [P, 512], F32))

        x_first_in = sem("x_first_in")
        weights_in, consts_in, rows_in = sem("weights_in"), sem("consts_in"), sem("rows_in")
        weights_split, consts_done, ones_set = sem("weights_split"), sem("consts_done"), sem("ones_set")
        bias_prod, bias_out_done = sem("bias_prod"), sem("bias_out_done")
        xc_in = [sem(f"xc_in{p}") for p in range(2)]
        x_in_loaded = [sem(f"x_in_loaded{p}") for p in range(2)]
        xc_hi_done, xc_lo_done = sem("xc_hi_done"), sem("xc_lo_done")
        qk_full, qk_raw_done = sem("qk_full"), sem("qk_raw_done")
        stack_full, stack_done = sem("stack_full"), sem("stack_done")
        v_full, v_done = sem("v_full"), sem("v_done")
        max_t_full = [sem(f"max_t_full{m}") for m in range(2)]
        max_t_done = [sem(f"max_t_done{m}") for m in range(2)]
        out_turn_full, context_done = sem("out_turn_full"), sem("context_done")
        ctx_turn_full, context_lo_done = sem("ctx_turn_full"), sem("context_lo_done")
        out_full, z_done = sem("out_full"), sem("z_done")
        qk_hi_done, qk_lo_done = sem("qk_hi_done"), sem("qk_lo_done")
        max_full, max_done = sem("max_full"), sem("max_done")
        neg_hi_done, neg_lo_done = sem("neg_hi_done"), sem("neg_lo_done")
        max_rows_in = [sem(f"max_rows_in{m}") for m in range(2)]
        score_full, exp_done = sem("score_full"), sem("exp_done")
        ctx_full, ctx_taken = sem("ctx_full"), sem("ctx_taken")
        inv_done, context_hi_done = sem("inv_done"), sem("context_hi_done")
        x_bias_done = sem("x_bias_done")
        stats_done, mean_var_done = sem("stats_done"), sem("mean_var_done")
        log_done, rstd_done = sem("log_done"), sem("rstd_done")
        norm_done, gamma_done, beta_done = sem("norm_done"), sem("gamma_done"), sem("beta_done")
        stored = [sem(f"stored{p}") for p in range(2)]

        block = ctx.enter_context(nc.Block())

        def norm(engine, ops, b, bp):
            for t in range(KT):
                ops.tensor_scalar(normed[bp][:, t, :], z[bp][:, t, :], mean_var[bp][:, t, 0:1], rstd[:, t:t + 1],
                                  ALU.subtract, ALU.mult).then_inc(norm_done, 1)
            engine.wait_ge(norm_done, KT * (b + 1))
            ops.tensor_tensor(normed[bp][:, :, :], normed[bp][:, :, :],
                              row_params[:, 1, :].unsqueeze(1).broadcast_to([P, KT, D]), ALU.mult).then_inc(gamma_done, 1)
            engine.wait_ge(gamma_done, b + 1)
            ops.tensor_tensor(normed[bp][:, :, :], normed[bp][:, :, :],
                              row_params[:, 2, :].unsqueeze(1).broadcast_to([P, KT, D]), ALU.add).then_inc(beta_done, 1)

        @block.sync
        def _(sp):
            def load_xc(b, par):
                wait(sp, xc_lo_done, 2 * (b - 1))
                sp.dma_start(xc_raw[par][:, 0], x_t[b].rearrange("(k p) s -> p k s", p=P)).then_inc(xc_in[par], 16)
                sp.dma_start(xc_raw[par][:, 1], c_t[b].rearrange("(k p) s -> p k s", p=P)).then_inc(xc_in[par], 16)

            def max_rows(b, par, half):
                wait(sp, max_t_done[half], b + 1)
                for side in range(2):
                    for part in range(2):
                        row, src = HALF * side + PARTS + part, (2 * side + part) * MP
                        sp.dma_start(stack[par][row:row + 1, MP * half:MP * (half + 1), 0, :].bitcast(F32),
                                     neg_max_t[half][src:src + MP, :].bitcast(F32)
                                     ).then_inc(max_rows_in[half], 16)

            def slot(n, par):
                if live(n - 1):
                    max_rows(n - 1, 1 - par, 1)
                if live(n + 3):
                    load_xc(n + 3, 1 - par)
                if live(n - 1):
                    wait(sp, z_done, n - 2)
                    sp.dma_start(x_in[1 - par][:, :, :], x[n - 1].rearrange("(t p) d -> p t d", p=P)
                                 ).then_inc(x_in_loaded[1 - par], 16)
                if live(n):
                    max_rows(n, par, 0)
                if live(n - 3):
                    wait(sp, beta_done, n - 2)
                    sp.dma_start(out[n - 3].rearrange("(t p) d -> p t d", p=P), normed[1 - par][:, :, :]
                                 ).then_inc(stored[1 - par], 16)

            w_rows = w.rearrange("(k p) a d -> p k a d", p=P)
            sp.dma_start(xc_raw[0][:, 0], x_t[0].rearrange("(k p) s -> p k s", p=P)).then_inc(x_first_in, 16)
            sp.dma_start(w_raw[:, :, 0:2, :], w_rows[:, :, 0:2, :]).then_inc(weights_in, 16)
            sp.dma_start(xc_raw[0][:, 1], c_t[0].rearrange("(k p) s -> p k s", p=P)).then_inc(xc_in[0], 16)
            sp.dma_start(bias_qk[:, :], b_q_k).then_inc(consts_in, 16)
            sp.dma_start(ones_rows[:, :], ones_rows_in).then_inc(consts_in, 16)
            sp.dma_start(sel_raw[:, :, :, :, :], select).then_inc(consts_in, 16)
            load_xc(1, 1)
            sp.dma_start(w_raw[:, :, 2:4, :], w_rows[:, :, 2:4, :]).then_inc(rows_in, 16)
            sp.dma_start(bias_v[:, :], b_v).then_inc(rows_in, 16)
            sp.dma_start(row_params[:, :, :], rows.unsqueeze(0).broadcast_to([P, 3, D])).then_inc(rows_in, 16)
            sp.dma_start(ident[:, :], ident_in).then_inc(rows_in, 16)
            slots(sp, slot)
            for p in range(2):
                sp.wait_ge(stored[p], 16 * B // 2)

        @block.tensor
        def _(pe):
            def three_passes(dst, stationary, moving):
                terms = [(a, c, k) for k in range(KT) for a, c in ((0, 0), (1, 0), (0, 1))]
                for t, (a, c, k) in enumerate(terms):
                    mm = nc.tensor.matmul(dst, stationary[a](k), moving[c](k), start=t == 0, stop=t == len(terms) - 1)
                return mm

            def bank_read(n, k):
                last = last_use(n, k)
                if last is None:
                    return
                b, what = last[0] + last[1][3], last[1][2]
                if what in ("qk0", "qk1"):
                    pe.wait_ge(qk_raw_done, 2 * b + int(what[2]) + 1)
                elif what == "stack":
                    pe.wait_ge(stack_done, PAIRS * b + last[1][5] + 1)
                elif what == "v":
                    pe.wait_ge(v_done, b + 1)
                elif what in ("max_turn0", "max_turn1"):
                    pe.wait_ge(max_t_done[int(what[8])], b + 1)
                elif what == "out_turn":
                    pe.wait_ge(context_done, KT * b + last[1][5] + 1)
                elif what == "ctx_turn":
                    pe.wait_ge(context_lo_done, b + 1)
                else:
                    pe.wait_ge(z_done, b + 1)

            def shared_work(k, use, n, par):
                b, what = n + use[3], use[2]
                if not live(b):
                    return
                bp = (par + use[3]) % 2
                ps = shared[use[4]]
                which = use[5]
                half_bank = ps[:, which * S:(which + 1) * S] if what in PROJECTIONS else None
                if what in ("qk0", "qk1"):
                    m = int(what[2])
                    pe.wait_ge(xc_lo_done, 2 * b + which + 1)
                    if which == 0:
                        bank_read(n, k)
                    mm = three_passes(half_bank, [lambda kt, t=t: t[:, kt, which, m * P:(m + 1) * P] for t in (w_hi, w_lo)],
                                      [lambda kt, t=t: t[bp][:, which, kt, :] for t in (xc_hi, xc_lo)])
                    if which == 1:
                        mm.then_inc(qk_full, 1)
                elif what == "stack":
                    pair = which
                    m, f, j = pair // MP, pair // 2 % 2, pair % 2
                    pe.wait_ge(qk_lo_done, 4 * b + 2 * m + f + 1)
                    bank_read(n, k)
                    for a in range(2):
                        mm = nc.tensor.matmul(ps[:, a * S:(a + 1) * S], sel[:, f, a, j, :], qk_parts[m][f][:, a, :],
                                              start=True, stop=True)
                    mm.then_inc(stack_full, 1)
                elif what == "v":
                    if which == 0:
                        bank_read(n, k)
                    mm = three_passes(half_bank,
                                      [lambda kt, u=u: u[bp][:, 1, kt, which * P:(which + 1) * P] for u in (xc_hi, xc_lo)],
                                      [lambda kt, u=u: u[:, kt, 2, :] for u in (w_hi, w_lo)])
                    if which == 1:
                        mm.then_inc(v_full, 1)
                elif what in ("max_turn0", "max_turn1"):
                    half = int(what[8])
                    pe.wait_ge(neg_lo_done, 2 * b + half + 1)
                    bank_read(n, k)
                    for t in range(KT):
                        mm = nc.tensor.transpose(ps[0:4 * MP, t * P:(t + 1) * P],
                                                 neg_max[half][:, t].rearrange("p e a j -> p (e a j)"), ident[:, :])
                    mm.then_inc(max_t_full[half], 1)
                elif what == "out_turn":
                    t = which
                    pe.wait_ge(ctx_taken, GROUPS * (b + 1))
                    bank_read(n, k)
                    for g in range(GROUPS):
                        mm = nc.tensor.transpose(ps[:, g * P:(g + 1) * P], ctx_t[bp][:, g, t * P:(t + 1) * P], ident[:, :])
                    mm.then_inc(out_turn_full, 1)
                elif what == "ctx_turn":
                    pe.wait_ge(context_done, KT * (b + 1))
                    bank_read(n, k)
                    for k2 in range(KT):
                        for t in range(KT):
                            mm = nc.tensor.transpose(ps[:, k2 * S + t * P:k2 * S + (t + 1) * P],
                                                     context[:, t, k2 * P:(k2 + 1) * P], ident[:, :])
                    mm.then_inc(ctx_turn_full, 1)
                else:
                    pe.wait_ge(context_lo_done, b + 1)
                    if which == 0:
                        bank_read(n, k)
                    mm = three_passes(half_bank,
                                      [lambda kt, u=u: u[:, kt, which * P:(which + 1) * P] for u in (context_hi, context_lo)],
                                      [lambda kt, u=u: u[:, kt, 3, :] for u in (w_hi, w_lo)])
                    if which == 1:
                        mm.then_inc(out_full, 1)

            def slot(n, par):
                for g in range(GROUPS):
                    for i in range(GH):
                        c, pair, base = GH * g + i, 2 * g + i // 2, HALF * (i % 2)
                        if live(n):
                            if i % 2 == 0:
                                pe.wait_ge(stack_done, PAIRS * n + pair + 1)
                            wait(pe, max_done, H * n + c - 1)
                            for t in range(KT):
                                mm = nc.tensor.matmul(max_ps[c % 2][:, t, :],
                                                      stack[par][base:base + PARTS, pair, 0, t * P:(t + 1) * P],
                                                      stack[par][base:base + PARTS, pair, 1, :], start=True, stop=True)
                            mm.then_inc(max_full, 1)
                        if live(n - 1):
                            if g % 2 == 0 and i == 0:
                                pe.wait_ge(max_rows_in[g // 2], 64 * n)
                            wait(pe, exp_done, H * (n - 1) + c - 1)
                            for t in range(KT):
                                mm = nc.tensor.matmul(score_ps[c % 2][:, t, :],
                                                      stack[1 - par][base:base + ROWS, pair, 1, t * P:(t + 1) * P],
                                                      stack[1 - par][base:base + ROWS, pair, 0, :], start=True, stop=True)
                            mm.then_inc(score_full, 1)
                        if i % 2 == 1:
                            b, vg, bp = (n - 2, GROUPS - 1, par) if g == 0 else (n - 1, g - 1, 1 - par)
                            if live(b):
                                group = GROUPS * b + vg
                                t = i // 2
                                if t == 0:
                                    pe.wait_ge(exp_done, GH * (group + 1))
                                    pe.wait_ge(v_done, b + 1)
                                    wait(pe, ctx_taken, group)
                                for j in range(GH):
                                    mm = nc.tensor.matmul(ctx_ps[32 * j:32 * j + 32, 0:S],
                                                          v_ones[bp][:, t, GH * vg + j, :],
                                                          probs[:, GH * (vg % 2) + j, t, :],
                                                          start=t == 0, stop=t == KT - 1)
                                if t == KT - 1:
                                    mm.then_inc(ctx_full, 1)
                        for k, use in uses_at(g, i):
                            shared_work(k, use, n, par)

            def bias_product():
                pe.wait_ge(consts_done, 2)
                for kt in range(KT):
                    mm = nc.tensor.matmul(ctx_ps[:, 0:D], bias_v_wide[:, kt, :], w_raw[:, kt, 3, :],
                                          start=kt == 0, stop=kt == KT - 1)
                mm.then_inc(bias_prod, 1)

            pe.wait_ge(weights_split, 2)
            pe.wait_ge(consts_done, 1)
            slots(pe, slot, bias_product)

        @block.scalar
        def _(act):
            def shared_read(k, use, n, par):
                b, what = n + use[3], use[2]
                if not live(b) or what in ("out_turn", "out_proj"):
                    return
                if what in PROJECTIONS and use[5] == 0:
                    return
                bp = (par + use[3]) % 2
                ps = shared[use[4]]
                if what in ("qk0", "qk1"):
                    m = int(what[2])
                    act.wait_ge(qk_full, 2 * b + m + 1)
                    nc.scalar.activation(qk_raw[m][:, 0, :], ps[:, 0:S], ACT.Identity, bias=bias_qk[:, 2 * m:2 * m + 1])
                    nc.scalar.activation(qk_raw[m][:, 1, :], ps[:, S:2 * S], ACT.Identity,
                                         bias=bias_qk[:, 2 * m + 1:2 * m + 2]).then_inc(qk_raw_done, 1)
                elif what == "stack":
                    act.wait_ge(stack_full, PAIRS * b + use[5] + 1)
                    nc.scalar.activation(stack[bp][:, use[5], :, :].rearrange("p a s -> p (a s)"), ps[:, :], ACT.Identity,
                                         bias=ones_rows[:, 0:1]).then_inc(stack_done, 1)
                elif what == "v":
                    act.wait_ge(v_full, b + 1)
                    nc.scalar.copy(v_ones[bp][:, :, :, 0:DK].rearrange("p t h d -> p (t h) d"),
                                   ps[:, :].rearrange("p (h d) -> p h d", d=DK)).then_inc(v_done, 1)
                elif what in ("max_turn0", "max_turn1"):
                    half = int(what[8])
                    act.wait_ge(max_t_full[half], b + 1)
                    wait(act, max_rows_in[half], 64 * b)
                    nc.scalar.copy(neg_max_t[half][:, :], ps[0:4 * MP, 0:S]).then_inc(max_t_done[half], 1)
                else:
                    act.wait_ge(ctx_turn_full, b + 1)
                    nc.scalar.copy(context_hi[:, :, :].rearrange("p k s -> p (k s)"), ps[:, :]).then_inc(context_hi_done, 1)

            def slot(n, par):
                for g in range(GROUPS):
                    for i in range(GH):
                        c = GH * g + i
                        if live(n - 1):
                            act.wait_ge(score_full, H * (n - 1) + c + 1)
                            nc.scalar.activation(probs[:, GH * (g % 2) + i, :, :], score_ps[c % 2][:, :, :], ACT.Exp,
                                                 scale=SCALE).then_inc(exp_done, 1)
                        if i == 3:
                            b, vg, bp = (n - 2, GROUPS - 1, par) if g == 0 else (n - 1, g - 1, 1 - par)
                            if live(b):
                                act.wait_ge(ctx_full, GROUPS * b + vg + 1)
                                nc.scalar.copy(ctx_t[bp][:, vg, :], ctx_ps[:, 0:S]).then_inc(ctx_taken, 1)
                        for k, use in uses_at(g, i):
                            shared_read(k, use, n, par)
                        if (g, i) == (0, 1) and live(n - 3):
                            act.wait_ge(mean_var_done, KT * (n - 2))
                            wait(act, norm_done, KT * (n - 3))
                            nc.scalar.activation(log_var[:, :], mean_var[1 - par][:, :, 1], ACT.Ln,
                                                 bias=eps_col[:, 0:1]).then_inc(log_done, 1)
                            act.wait_ge(log_done, n - 2)
                            nc.scalar.activation(rstd[:, :], log_var[:, :], ACT.Exp, scale=-0.5).then_inc(rstd_done, 1)

            nc.scalar.preload_act_table_set("natural_log_exp_and_others")
            act.wait_ge(consts_in, 48)
            act.wait_ge(ones_set, 3)
            slots(act, slot)

        @block.vector
        def _(dve):
            def negate(n, half):
                hi, lo = neg_max[half][:, :, :, 0, :], neg_max[half][:, :, :, 1, :]
                top = row_max[:, :, :, MP * half:MP * (half + 1)]
                dve.wait_ge(max_done, H * n + H // 2 * (half + 1))
                nc.vector.tensor_scalar(hi.bitcast(F32R), top, -1.0, None, ALU.mult).then_inc(neg_hi_done, 1)
                dve.wait_ge(neg_hi_done, 2 * n + half + 1)
                nc.vector.scalar_tensor_tensor(out=lo, in0=top, scalar=-1.0, in1=hi, op0=ALU.mult,
                                               op1=ALU.subtract).then_inc(neg_lo_done, 1)

            def divide(b, t, bank):
                heads = shared[bank][:, :].rearrange("p (h c) -> p h c", c=2 * DK)
                dve.wait_ge(out_turn_full, KT * b + t + 1)
                nc.vector.reciprocal(inv_sum[:, t, :], heads[:, :, DK]).then_inc(inv_done, 1)
                dve.wait_ge(inv_done, KT * b + t + 1)
                nc.vector.tensor_tensor(context[:, t, :].rearrange("p (h d) -> p h d", d=DK), heads[:, :, 0:DK],
                                        inv_sum[:, t, :].unsqueeze(2).broadcast_to([P, H, DK]),
                                        ALU.mult).then_inc(context_done, 1)

            def split_qk_lo(b, m):
                for f in range(2):
                    rows, others = slice(HALF * f, HALF * (f + 1)), slice(HALF * (1 - f), HALF * (2 - f))
                    dve.wait_ge(qk_hi_done, 4 * b + 2 * m + f + 1)
                    nc.vector.tensor_tensor(qk_parts[m][f][others, :, :], qk_raw[m][rows, :, :],
                                            qk_parts[m][f][rows, :, :], ALU.subtract).then_inc(qk_lo_done, 1)

            QK_LO_AT = [(1, 1), (2, 2)]
            bank = {(use[2], use[5]): use[4] for use in SHARED}

            def slot(n, par):
                for g in range(GROUPS):
                    for i in range(GH):
                        c = GH * g + i
                        b = n - 2
                        if (g, i) == (0, 0) and live(n - 3):
                            dve.wait_ge(stats_done, KT * (n - 2))
                        if live(n):
                            dve.wait_ge(max_full, H * n + c + 1)
                            nc.vector.tensor_reduce(row_max[:, :, i % 2, 2 * g + i // 2], max_ps[c % 2][:, :, :], AX.X,
                                                    ALU.max).then_inc(max_done, 1)
                            if (g, i) in ((1, 3), (3, 3)):
                                negate(n, g // 2)
                        if (g, i) == (0, 0) and live(n - 3):
                            for t in range(KT):
                                nc.vector.bn_aggr(mean_var[1 - par][:, t, :], stats[:, t, :]).then_inc(mean_var_done, 1)
                        if (g, i) == (0, 1) and is_last(n - 3):
                            dve.wait_ge(rstd_done, B)
                            dve.wait_ge(stored[1 - par], 8 * (n - 3 - (1 - par)))
                            dve.wait_ge(beta_done, B - 1)
                            norm(dve, nc.vector, n - 3, 1 - par)
                        if (g, i) in ((1, 0), (1, 2)) and live(b):
                            divide(b, i // 2, bank["out_turn", i // 2])
                        if (g, i) == (2, 1) and live(b):
                            dve.wait_ge(context_hi_done, b + 1)
                            nc.vector.tensor_tensor(context_lo[:, :, :].rearrange("p k s -> p (k s)"),
                                                    shared[bank["ctx_turn", 0]][:, :],
                                                    context_hi[:, :, :].rearrange("p k s -> p (k s)"),
                                                    ALU.subtract).then_inc(context_lo_done, 1)
                        if (g, i) in QK_LO_AT and live(n + 1):
                            split_qk_lo(n + 1, QK_LO_AT.index((g, i)))
                        if (g, i) == (3, 2) and live(b):
                            dve.wait_ge(out_full, b + 1)
                            dve.wait_ge(x_bias_done, b + 1)
                            wait(dve, norm_done, KT * (b - 1))
                            nc.vector.tensor_tensor(z[par][:, :, :].rearrange("p t d -> p (t d)"),
                                                    shared[bank["out_proj", 0]][:, :],
                                                    x_in[par][:, :, :].rearrange("p t d -> p (t d)"),
                                                    ALU.add).then_inc(z_done, 1)
                        if (g, i) == (3, 3) and live(b):
                            dve.wait_ge(z_done, b + 1)
                            for t in range(KT):
                                nc.vector.bn_stats(stats[:, t, :], z[par][:, t, :]).then_inc(stats_done, 1)

            def split_weights(matrices, count):
                nc.vector.tensor_copy(w_hi[:, :, matrices, :], w_raw[:, :, matrices, :]).then_inc(weights_split, 1)
                dve.wait_ge(weights_split, count + 1)
                nc.vector.tensor_tensor(w_lo[:, :, matrices, :], w_raw[:, :, matrices, :], w_hi[:, :, matrices, :],
                                        ALU.subtract).then_inc(weights_split, 1)

            def rest_of_constants():
                dve.wait_ge(rows_in, 64)
                nc.vector.tensor_copy(bias_v_wide[:, :, :], bias_v[:, :].unsqueeze(2).broadcast_to([P, KT, P])
                                      ).then_inc(consts_done, 1)
                split_weights(slice(2, 4), 2)
                dve.wait_ge(bias_prod, 1)
                nc.vector.tensor_tensor(bias_out[:, :], ctx_ps[:, 0:D], row_params[:, 0, :],
                                        ALU.add).then_inc(bias_out_done, 1)

            dve.wait_ge(weights_in, 16)
            split_weights(slice(0, 2), 0)
            dve.wait_ge(consts_in, 48)
            nc.vector.tensor_copy(sel[:, :, :, :, :], sel_raw[:, :, :, :, :]).then_inc(consts_done, 1)
            slots(dve, slot, rest_of_constants)

        @block.gpsimd
        def _(pool):
            def split_xc(b, bp, a):
                if not isinstance(b, int) or b > 0:
                    wait(pool, xc_in[bp], 16 * (b - bp) + 32 - 16 * (1 - bp))
                else:
                    pool.wait_ge(xc_in[0] if a else x_first_in, 16)
                if a == 1:
                    wait(pool, v_full, b - 1)
                nc.gpsimd.tensor_tensor(xc_hi[bp][:, a], xc_raw[bp][:, a],
                                        one_col[:, :].unsqueeze(2).broadcast_to([P, KT, S]),
                                        ALU.mult).then_inc(xc_hi_done, 1)
                pool.wait_ge(xc_hi_done, 2 * b + a + 1)
                nc.gpsimd.tensor_tensor(xc_lo[bp][:, a], xc_raw[bp][:, a], xc_hi[bp][:, a],
                                        ALU.subtract).then_inc(xc_lo_done, 1)

            def split_qk_hi(b, m):
                for f in range(2):
                    if f == 0:
                        wait(pool, qk_raw_done, 2 * b + m + 1)
                    nc.gpsimd.tensor_tensor(qk_parts[m][f][:, :, :], qk_raw[m][:, :, :],
                                            one_col[:, :].unsqueeze(2).broadcast_to([P, 2, S]),
                                            ALU.mult).then_inc(qk_hi_done, 1)

            def slot(n, par):
                if live(n + 1):
                    split_qk_hi(n + 1, 0)
                    if not live(n):
                        split_qk_hi(n + 1, 1)
                if live(n - 2):
                    pool.wait_ge(x_in_loaded[par], 8 * (n - 2 - par) + 16)
                    nc.gpsimd.tensor_tensor(x_in[par][:, :, :], x_in[par][:, :, :],
                                            bias_out[:, :].unsqueeze(1).broadcast_to([P, KT, D]),
                                            ALU.add).then_inc(x_bias_done, 1)
                if live(n + 2):
                    split_xc(n + 2, par, 0)
                if live(n - 3) and not is_last(n - 3):
                    pool.wait_ge(rstd_done, n - 2)
                    wait(pool, stored[1 - par], 8 * (n - 3 - (1 - par)))
                if live(n + 1) and live(n):
                    split_qk_hi(n + 1, 1)
                if live(n - 3) and not is_last(n - 3):
                    norm(pool, nc.gpsimd, n - 3, 1 - par)
                if live(n + 2):
                    split_xc(n + 2, par, 1)

            for p in range(2):
                nc.gpsimd.memset(v_ones[p][:, :, :, :], 1.0).then_inc(ones_set, 1)
            nc.gpsimd.memset(eps_col[:, :], EPS).then_inc(ones_set, 1)
            nc.gpsimd.memset(one_col[:, :], 1.0).then_inc(ones_set, 1)
            pool.wait_ge(ones_set, 4)
            for a in range(2):
                split_xc(0, 0, a)
            slots(pool, slot, lambda: pool.wait_ge(bias_out_done, 1))


def kernel(x, ctx_1024, L0_xattn_W_qkv, L0_xattn_b_qkv, L0_xattn_W_o, L0_xattn_b_o, L0_xattn_ln_gamma, L0_xattn_ln_beta):
    import numpy as np
    from concourse import bacc
    from concourse.bass_utils import run_bass_kernel_spmd

    x, c = np.asarray(x), np.asarray(ctx_1024)
    w_qkv, w_o = np.asarray(L0_xattn_W_qkv), np.asarray(L0_xattn_W_o)
    b_qkv = np.asarray(L0_xattn_b_qkv)

    w = np.stack([w_qkv[:D].T, w_qkv[D:2 * D].T, w_qkv[2 * D:].T, w_o.T], axis=1)
    b_q_k = np.stack([b_qkv[a * D:(a + 1) * D][m * P:(m + 1) * P] for m in range(KT) for a in range(2)], axis=1)

    select = np.zeros((P, 2, 2, 2, P), np.float32)
    for a, (hi_places, lo_place) in enumerate((((0, 2), 1), ((0, 1), 2))):
        for f in range(2):
            for j in range(2):
                for side in range(2):
                    for d in range(DK):
                        feature = 2 * DK * j + DK * side + d
                        for place in hi_places:
                            select[HALF * f + feature, f, a, j, HALF * side + DK * place + d] = 1
                        select[HALF * (1 - f) + feature, f, a, j, HALF * side + DK * lo_place + d] = 1
    ones_rows = np.zeros((P, 1), np.float32)
    for side in range(2):
        ones_rows[HALF * side + PARTS:HALF * side + ROWS] = 1

    arrays = {
        "x_t": x.transpose(0, 2, 1), "c_t": c.transpose(0, 2, 1), "x": x, "w": w, "b_q_k": b_q_k, "b_v": b_qkv[2 * D:].reshape(KT, P).T,
        "rows": np.stack([np.asarray(L0_xattn_b_o), np.asarray(L0_xattn_ln_gamma), np.asarray(L0_xattn_ln_beta)]),
        "select": select, "ident": np.eye(P, dtype=np.float32), "ones_rows": ones_rows,
    }
    arrays = {f"in_{name}": np.ascontiguousarray(a) for name, a in arrays.items()}
    nc = bacc.Bacc("TRN2", target_bir_lowering=False, num_devices=1)
    args = [nc.dram_tensor(name, a.shape, mybir.dt.from_np(a.dtype), kind="ExternalInput").ap() for name, a in arrays.items()]
    args.append(nc.dram_tensor("out", (B, S, D), F32, kind="ExternalOutput").ap())
    xattn_kernel(nc, *args)
    return run_bass_kernel_spmd(nc, [arrays], core_ids=[0]).results[0]["out"]
```

```python
from contextlib import ExitStack

import concourse.bass as bass
from concourse import mybir

F32 = mybir.dt.float32
F32R = mybir.dt.float32r
ALU = mybir.AluOpType
ACT = mybir.ActivationFunctionType
AX = mybir.AxisListType

P = 128
B = 32
S = 256
D = 256
H = 16
DK = D // H
KT = D // P
GROUPS = 4
GH = H // GROUPS
PAIRS = H // 2
MP = PAIRS // KT
HALF = 64
PARTS = 3 * DK
ROWS = PARTS + 2
EPS = 1e-5
SCALE = 1.0 / DK ** 0.5

BANKS = 3
SHARED = [
    (0, 0, "max_turn1", -1, 1, 0), (0, 0, "qk0", 1, 0, 0),
    (0, 1, "stack", 0, 2, 6), (0, 1, "stack", 0, 1, 7),
    (1, 0, "qk1", 1, 0, 0), (1, 0, "out_turn", -2, 2, 0), (1, 0, "out_turn", -2, 1, 1),
    (1, 1, "stack", 1, 0, 0),
    (2, 0, "max_turn0", 0, 0, 0), (2, 0, "v", 0, 2, 0), (2, 0, "ctx_turn", -2, 1, 0),
    (2, 1, "stack", 1, 0, 1), (2, 1, "stack", 1, 2, 2),
    (3, 0, "out_proj", -2, 1, 0), (3, 0, "stack", 1, 2, 3),
    (3, 1, "stack", 1, 0, 4), (3, 1, "stack", 1, 2, 5),
]
FIRST_SLOT, LAST_SLOT = -1, B + 2
LOOP_FROM, LOOP_TO = 4, B - 4


def live(batch):
    return not isinstance(batch, int) or 0 <= batch < B


def is_last(batch):
    return isinstance(batch, int) and batch == B - 1


def uses_at(g, p):
    return [(k, use) for k, use in enumerate(SHARED) if use[:2] == (g, p)]


def bank_at(n, k):
    if isinstance(n, int) and n < 2:
        return sum(live(n + use[3]) for use in SHARED[:k]) % BANKS
    return SHARED[k][4]


def last_use(n, k):
    slot, bank = n, bank_at(n, k)
    while True:
        k -= 1
        if k < 0:
            slot, k = slot - 1, len(SHARED) - 1
        if isinstance(slot, int) and slot < FIRST_SLOT:
            return None
        if bank_at(slot, k) == bank and live(slot + SHARED[k][3]):
            return slot, SHARED[k]


def wait(eng, sem, value):
    if not isinstance(value, int) or value > 0:
        eng.wait_ge(sem, value)


def slots(eng, slot, after_slot_0=None):
    for n in range(FIRST_SLOT, LOOP_FROM):
        slot(n, n % 2)
        if n == 0 and after_slot_0:
            after_slot_0()
    with eng.Fori(LOOP_FROM, LOOP_TO, 2) as n:
        slot(n, 0)
        slot(n + 1, 1)
    for n in range(LOOP_TO, LAST_SLOT + 1):
        slot(n, n % 2)


def xattn_kernel(nc, x_t, c_t, x, w, b_q_k, b_v, rows, select, ident_in, ones_rows_in, out):
    with ExitStack() as ctx:
        def sb(name, shape, dt=F32):
            return ctx.enter_context(nc.sbuf_tensor(name, shape, dt))

        def sem(name):
            return ctx.enter_context(nc.semaphore(name))

        w_raw = sb("w_raw", [P, KT, 4, D])
        w_hi = sb("w_hi", [P, KT, 4, D], F32R)
        w_lo = sb("w_lo", [P, KT, 4, D], F32R)
        sel_raw = sb("sel_raw", [P, 2, 2, 2, P])
        sel = sb("sel", [P, 2, 2, 2, P], F32R)
        bias_qk = sb("bias_qk", [P, 2 * KT])
        bias_v = sb("bias_v", [P, KT])
        bias_v_wide = sb("bias_v_wide", [P, KT, P])
        row_params = sb("row_params", [P, 3, D])
        bias_out = sb("bias_out", [P, D])
        ident = sb("ident", [P, P])
        ident_r = sb("ident_r", [P, P], F32R)
        ones_rows = sb("ones_rows", [P, 1])
        xc_raw = [sb(f"xc_raw{p}", [P, 2, KT, S]) for p in range(2)]
        xc_hi = [sb(f"xc_hi{p}", [P, 2, KT, S], F32R) for p in range(2)]
        xc_lo = [sb(f"xc_lo{p}", [P, 2, KT, S], F32R) for p in range(2)]
        qk_raw = [sb(f"qk_raw{m}", [P, 2, S]) for m in range(KT)]
        qk_parts = [[sb(f"qk_parts{m}{f}", [P, 2, S], F32R) for f in range(2)] for m in range(KT)]
        stack = [sb(f"stack{p}", [P, PAIRS, 2, S], F32R) for p in range(2)]
        v_ones = [sb(f"v_ones{p}", [P, KT, H, 2 * DK]) for p in range(2)]
        row_max = sb("row_max", [P, KT, 2, PAIRS])
        neg_max = [sb(f"neg_max{m}", [P, KT, 2, 2, MP], F32R) for m in range(2)]
        neg_max_t = [sb(f"neg_max_t{m}", [4 * MP, S], F32R) for m in range(2)]
        probs = sb("probs", [P, 2 * GH, KT, S])
        ctx_t = [sb(f"ctx_t{p}", [P, GROUPS, S]) for p in range(2)]
        inv_sum = sb("inv_sum", [P, KT, H])
        context = sb("context", [P, KT, D])
        context_hi = sb("context_hi", [P, KT, S], F32R)
        context_lo = sb("context_lo", [P, KT, S], F32R)
        x_in = [sb(f"x_in{p}", [P, KT, D]) for p in range(2)]
        z = [sb(f"z{p}", [P, KT, D]) for p in range(2)]
        stats = sb("stats", [P, KT, 6])
        mean_var = [sb(f"mean_var{p}", [P, KT, 2]) for p in range(2)]
        log_var = sb("log_var", [P, KT])
        rstd = sb("rstd", [P, KT])
        eps_col = sb("eps_col", [P, 1])
        one_col = sb("one_col", [P, 1])
        normed = [sb(f"normed{p}", [P, KT, D]) for p in range(2)]

        shared = [ctx.enter_context(nc.psum_tensor(f"shared{k}", [P, 512], F32)) for k in range(BANKS)]
        max_ps = [ctx.enter_context(nc.psum_tensor(f"max_ps{k}", [P, KT, S], F32)) for k in range(2)]
        score_ps = [ctx.enter_context(nc.psum_tensor(f"score_ps{k}", [P, KT, S], F32)) for k in range(2)]
        ctx_ps = ctx.enter_context(nc.psum_tensor("ctx_ps", [P, 512], F32))

        x_first_in = sem("x_first_in")
        weights_rest_in = sem("weights_rest_in")
        weights_in, consts_in, rows_in = sem("weights_in"), sem("consts_in"), sem("rows_in")
        weights_split, consts_done, ones_set = sem("weights_split"), sem("consts_done"), sem("ones_set")
        bias_prod, bias_out_done = sem("bias_prod"), sem("bias_out_done")
        xc_in = [sem(f"xc_in{p}") for p in range(2)]
        x_in_loaded = [sem(f"x_in_loaded{p}") for p in range(2)]
        xc_hi_done, xc_lo_done = sem("xc_hi_done"), sem("xc_lo_done")
        qk_full, qk_raw_done = sem("qk_full"), sem("qk_raw_done")
        stack_full, stack_done = sem("stack_full"), sem("stack_done")
        v_full, v_done = sem("v_full"), sem("v_done")
        max_t_full = [sem(f"max_t_full{m}") for m in range(2)]
        max_t_done = [sem(f"max_t_done{m}") for m in range(2)]
        out_turn_full, context_done = sem("out_turn_full"), sem("context_done")
        ctx_turn_full, context_lo_done = sem("ctx_turn_full"), sem("context_lo_done")
        out_full, z_done = sem("out_full"), sem("z_done")
        qk_hi_done, qk_lo_done = sem("qk_hi_done"), sem("qk_lo_done")
        max_full, max_done = sem("max_full"), sem("max_done")
        neg_hi_done, neg_lo_done = sem("neg_hi_done"), sem("neg_lo_done")
        max_rows_in = [sem(f"max_rows_in{m}") for m in range(2)]
        score_full, exp_done = sem("score_full"), sem("exp_done")
        ctx_full, ctx_taken = sem("ctx_full"), sem("ctx_taken")
        inv_done, context_hi_done = sem("inv_done"), sem("context_hi_done")
        x_bias_done = sem("x_bias_done")
        stats_done, mean_var_done = sem("stats_done"), sem("mean_var_done")
        log_done, rstd_done = sem("log_done"), sem("rstd_done")
        norm_done, gamma_done, beta_done = sem("norm_done"), sem("gamma_done"), sem("beta_done")
        stored = [sem(f"stored{p}") for p in range(2)]

        block = ctx.enter_context(nc.Block())

        def norm(engine, ops, b, bp):
            for t in range(KT):
                ops.tensor_scalar(normed[bp][:, t, :], z[bp][:, t, :], mean_var[bp][:, t, 0:1], rstd[:, t:t + 1],
                                  ALU.subtract, ALU.mult).then_inc(norm_done, 1)
            engine.wait_ge(norm_done, KT * (b + 1))
            ops.tensor_tensor(normed[bp][:, :, :], normed[bp][:, :, :],
                              row_params[:, 1, :].unsqueeze(1).broadcast_to([P, KT, D]), ALU.mult).then_inc(gamma_done, 1)
            engine.wait_ge(gamma_done, b + 1)
            ops.tensor_tensor(normed[bp][:, :, :], normed[bp][:, :, :],
                              row_params[:, 2, :].unsqueeze(1).broadcast_to([P, KT, D]), ALU.add).then_inc(beta_done, 1)

        @block.sync
        def _(sp):
            def load_xc(b, par):
                wait(sp, xc_lo_done, 2 * (b - 1))
                sp.dma_start(xc_raw[par][:, 0], x_t[b].rearrange("(k p) s -> p k s", p=P)).then_inc(xc_in[par], 16)
                sp.dma_start(xc_raw[par][:, 1], c_t[b].rearrange("(k p) s -> p k s", p=P)).then_inc(xc_in[par], 16)

            def max_rows(b, par, half):
                wait(sp, max_t_done[half], b + 1)
                for side in range(2):
                    for part in range(2):
                        row, src = HALF * side + PARTS + part, (2 * side + part) * MP
                        sp.dma_start(stack[par][row:row + 1, MP * half:MP * (half + 1), 0, :].bitcast(F32),
                                     neg_max_t[half][src:src + MP, :].bitcast(F32)
                                     ).then_inc(max_rows_in[half], 16)

            def slot(n, par):
                if live(n - 1):
                    max_rows(n - 1, 1 - par, 1)
                if live(n + 3):
                    load_xc(n + 3, 1 - par)
                if live(n - 1):
                    wait(sp, z_done, n - 2)
                    sp.dma_start(x_in[1 - par][:, :, :], x[n - 1].rearrange("(t p) d -> p t d", p=P)
                                 ).then_inc(x_in_loaded[1 - par], 16)
                if live(n):
                    max_rows(n, par, 0)
                if live(n - 3):
                    wait(sp, beta_done, n - 2)
                    sp.dma_start(out[n - 3].rearrange("(t p) d -> p t d", p=P), normed[1 - par][:, :, :]
                                 ).then_inc(stored[1 - par], 16)

            w_rows = w.rearrange("(k p) a d -> p k a d", p=P)
            sp.dma_start(xc_raw[0][:, 0], x_t[0].rearrange("(k p) s -> p k s", p=P)).then_inc(x_first_in, 16)
            sp.dma_start(w_raw[:, :, 0:2, :], w_rows[:, :, 0:2, :]).then_inc(weights_in, 16)
            sp.dma_start(xc_raw[0][:, 1], c_t[0].rearrange("(k p) s -> p k s", p=P)).then_inc(xc_in[0], 16)
            sp.dma_start(bias_qk[:, :], b_q_k).then_inc(consts_in, 16)
            sp.dma_start(ones_rows[:, :], ones_rows_in).then_inc(consts_in, 16)
            sp.dma_start(sel_raw[:, :, :, :, :], select).then_inc(consts_in, 16)
            load_xc(1, 1)
            sp.dma_start(w_raw[:, :, 2:4, :], w_rows[:, :, 2:4, :]).then_inc(weights_rest_in, 16)
            sp.dma_start(bias_v[:, :], b_v).then_inc(rows_in, 16)
            sp.dma_start(row_params[:, :, :], rows.unsqueeze(0).broadcast_to([P, 3, D])).then_inc(rows_in, 16)
            sp.dma_start(ident[:, :], ident_in).then_inc(rows_in, 16)
            slots(sp, slot)
            for p in range(2):
                sp.wait_ge(stored[p], 16 * B // 2)

        @block.tensor
        def _(pe):
            def three_passes(dst, stationary, moving):
                terms = [(a, c, k) for k in range(KT) for a, c in ((0, 0), (1, 0), (0, 1))]
                for t, (a, c, k) in enumerate(terms):
                    mm = nc.tensor.matmul(dst, stationary[a](k), moving[c](k), start=t == 0, stop=t == len(terms) - 1)
                return mm

            def bank_read(n, k):
                last = last_use(n, k)
                if last is None:
                    return
                b, what = last[0] + last[1][3], last[1][2]
                if what in ("qk0", "qk1"):
                    pe.wait_ge(qk_raw_done, 2 * b + int(what[2]) + 1)
                elif what == "stack":
                    pe.wait_ge(stack_done, PAIRS * b + last[1][5] + 1)
                elif what == "v":
                    pe.wait_ge(v_done, b + 1)
                elif what in ("max_turn0", "max_turn1"):
                    pe.wait_ge(max_t_done[int(what[8])], b + 1)
                elif what == "out_turn":
                    pe.wait_ge(context_done, KT * b + last[1][5] + 1)
                elif what == "ctx_turn":
                    pe.wait_ge(context_lo_done, b + 1)
                else:
                    pe.wait_ge(z_done, b + 1)

            def shared_work(k, use, n, par):
                b, what = n + use[3], use[2]
                if not live(b):
                    return
                bp = (par + use[3]) % 2
                ps = shared[bank_at(n, k)]
                if what in ("qk0", "qk1"):
                    m = int(what[2])
                    pe.wait_ge(xc_lo_done, 2 * (b + 1))
                    bank_read(n, k)
                    for a in range(2):
                        mm = three_passes(ps[:, a * S:(a + 1) * S],
                                          [lambda kt, a=a, t=t: t[:, kt, a, m * P:(m + 1) * P] for t in (w_hi, w_lo)],
                                          [lambda kt, a=a, t=t: t[bp][:, a, kt, :] for t in (xc_hi, xc_lo)])
                    mm.then_inc(qk_full, 1)
                elif what == "stack":
                    pair = use[5]
                    m, f, j = pair // MP, pair // 2 % 2, pair % 2
                    pe.wait_ge(qk_lo_done, 4 * b + 2 * m + f + 1)
                    bank_read(n, k)
                    for a in range(2):
                        mm = nc.tensor.matmul(ps[:, a * S:(a + 1) * S], sel[:, f, a, j, :], qk_parts[m][f][:, a, :],
                                              start=True, stop=True)
                    mm.then_inc(stack_full, 1)
                elif what == "v":
                    bank_read(n, k)
                    for t in range(KT):
                        mm = three_passes(ps[:, t * D:(t + 1) * D],
                                          [lambda kt, t=t, u=u: u[bp][:, 1, kt, t * P:(t + 1) * P] for u in (xc_hi, xc_lo)],
                                          [lambda kt, u=u: u[:, kt, 2, :] for u in (w_hi, w_lo)])
                    mm.then_inc(v_full, 1)
                elif what in ("max_turn0", "max_turn1"):
                    half = int(what[8])
                    pe.wait_ge(neg_lo_done, 2 * b + half + 1)
                    bank_read(n, k)
                    for t in range(KT):
                        mm = nc.tensor.matmul(ps[0:4 * MP, t * P:(t + 1) * P],
                                              neg_max[half][:, t].rearrange("p e a j -> p (e a j)"), ident_r[:, :],
                                              start=True, stop=True)
                    mm.then_inc(max_t_full[half], 1)
                elif what == "out_turn":
                    t = use[5]
                    pe.wait_ge(ctx_taken, GROUPS * (b + 1))
                    bank_read(n, k)
                    for g in range(GROUPS):
                        mm = nc.tensor.transpose(ps[:, g * P:(g + 1) * P], ctx_t[bp][:, g, t * P:(t + 1) * P], ident[:, :])
                    mm.then_inc(out_turn_full, 1)
                elif what == "ctx_turn":
                    pe.wait_ge(context_done, KT * (b + 1))
                    bank_read(n, k)
                    for k2 in range(KT):
                        for t in range(KT):
                            mm = nc.tensor.transpose(ps[:, k2 * S + t * P:k2 * S + (t + 1) * P],
                                                     context[:, t, k2 * P:(k2 + 1) * P], ident[:, :])
                    mm.then_inc(ctx_turn_full, 1)
                else:
                    pe.wait_ge(context_lo_done, b + 1)
                    bank_read(n, k)
                    for t in range(KT):
                        mm = three_passes(ps[:, t * D:(t + 1) * D],
                                          [lambda kt, t=t, u=u: u[:, kt, t * P:(t + 1) * P] for u in (context_hi, context_lo)],
                                          [lambda kt, u=u: u[:, kt, 3, :] for u in (w_hi, w_lo)])
                    mm.then_inc(out_full, 1)

            def products_with_v(n, par, g):
                b, vg, bp = (n - 2, GROUPS - 1, par) if g == 0 else (n - 1, g - 1, 1 - par)
                if not live(b):
                    return
                group = GROUPS * b + vg
                pe.wait_ge(exp_done, GH * (group + 1))
                pe.wait_ge(v_done, b + 1)
                wait(pe, ctx_taken, group)
                for t in range(KT):
                    for j in range(GH):
                        mm = nc.tensor.matmul(ctx_ps[32 * j:32 * j + 32, 0:S], v_ones[bp][:, t, GH * vg + j, :],
                                              probs[:, GH * (vg % 2) + j, t, :], start=t == 0, stop=t == KT - 1)
                mm.then_inc(ctx_full, 1)

            turns = [(t, side) for t in range(KT) for side in range(2)]

            def slot(n, par):
                for g in range(GROUPS):
                    for p in range(2):
                        pair = 2 * g + p
                        uses = uses_at(g, p)
                        if p == 1 and len(uses) == 2:
                            shared_work(*uses.pop(0), n, par)
                        if live(n):
                            pe.wait_ge(stack_done, PAIRS * n + pair + 1)
                            if live(n - 1):
                                wait(pe, max_done, H * n + 2 * pair)
                            for t, side in turns if live(n - 1) else sorted(turns, key=lambda turn: turn[1]):
                                if not live(n - 1) and t == 0:
                                    wait(pe, max_done, 2 * pair + side - 1)
                                rows = slice(HALF * side, HALF * side + PARTS)
                                mm = nc.tensor.matmul(max_ps[side][:, t, :], stack[par][rows, pair, 0, t * P:(t + 1) * P],
                                                      stack[par][rows, pair, 1, :], start=True, stop=True)
                                if t == KT - 1:
                                    mm.then_inc(max_full, 1)
                        if live(n - 1):
                            if p == 0 and g % 2 == 0:
                                pe.wait_ge(max_rows_in[g // 2], 64 * n)
                            wait(pe, exp_done, H * (n - 1) + 2 * pair)
                            last = stack[1 - par]
                            for t, side in turns:
                                rows = slice(HALF * side, HALF * side + ROWS)
                                mm = nc.tensor.matmul(score_ps[side][:, t, :], last[rows, pair, 1, t * P:(t + 1) * P],
                                                      last[rows, pair, 0, :], start=True, stop=True)
                                if t == KT - 1:
                                    mm.then_inc(score_full, 1)
                        if p == 1:
                            products_with_v(n, par, g)
                        for k, use in uses:
                            shared_work(k, use, n, par)

            def bias_product():
                pe.wait_ge(consts_done, 3)
                for kt in range(KT):
                    mm = nc.tensor.matmul(ctx_ps[:, 0:D], bias_v_wide[:, kt, :], w_raw[:, kt, 3, :],
                                          start=kt == 0, stop=kt == KT - 1)
                mm.then_inc(bias_prod, 1)

            pe.wait_ge(weights_split, 2)
            pe.wait_ge(consts_done, 1)
            slots(pe, slot, bias_product)

        @block.scalar
        def _(act):
            def shared_read(k, use, n, par):
                b, what = n + use[3], use[2]
                if not live(b) or what in ("out_turn", "out_proj"):
                    return
                bp = (par + use[3]) % 2
                ps = shared[bank_at(n, k)]
                if what in ("qk0", "qk1"):
                    m = int(what[2])
                    act.wait_ge(qk_full, 2 * b + m + 1)
                    nc.scalar.activation(qk_raw[m][:, 0, :], ps[:, 0:S], ACT.Identity, bias=bias_qk[:, 2 * m:2 * m + 1])
                    nc.scalar.activation(qk_raw[m][:, 1, :], ps[:, S:2 * S], ACT.Identity,
                                         bias=bias_qk[:, 2 * m + 1:2 * m + 2]).then_inc(qk_raw_done, 1)
                elif what == "stack":
                    act.wait_ge(stack_full, PAIRS * b + use[5] + 1)
                    nc.scalar.activation(stack[bp][:, use[5], :, :].rearrange("p a s -> p (a s)"), ps[:, :], ACT.Identity,
                                         bias=ones_rows[:, 0:1]).then_inc(stack_done, 1)
                elif what == "v":
                    act.wait_ge(v_full, b + 1)
                    nc.scalar.copy(v_ones[bp][:, :, :, 0:DK].rearrange("p t h d -> p (t h) d"),
                                   ps[:, :].rearrange("p (h d) -> p h d", d=DK)).then_inc(v_done, 1)
                elif what in ("max_turn0", "max_turn1"):
                    half = int(what[8])
                    act.wait_ge(max_t_full[half], b + 1)
                    wait(act, max_rows_in[half], 64 * b)
                    nc.scalar.copy(neg_max_t[half][:, :], ps[0:4 * MP, 0:S]).then_inc(max_t_done[half], 1)
                else:
                    act.wait_ge(ctx_turn_full, b + 1)
                    nc.scalar.copy(context_hi[:, :, :].rearrange("p k s -> p (k s)"), ps[:, :]).then_inc(context_hi_done, 1)

            def slot(n, par):
                for g in range(GROUPS):
                    for p in range(2):
                        uses = uses_at(g, p)
                        if p == 1 and len(uses) == 2:
                            shared_read(*uses.pop(0), n, par)
                        for side in range(2):
                            c = GH * g + 2 * p + side
                            if live(n - 1):
                                act.wait_ge(score_full, H * (n - 1) + c + 1)
                                nc.scalar.activation(probs[:, GH * (g % 2) + 2 * p + side, :, :], score_ps[side][:, :, :],
                                                     ACT.Exp, scale=SCALE).then_inc(exp_done, 1)
                        if p == 1:
                            b, vg, bp = (n - 2, GROUPS - 1, par) if g == 0 else (n - 1, g - 1, 1 - par)
                            if live(b):
                                act.wait_ge(ctx_full, GROUPS * b + vg + 1)
                                nc.scalar.copy(ctx_t[bp][:, vg, :], ctx_ps[:, 0:S]).then_inc(ctx_taken, 1)
                        for k, use in uses:
                            shared_read(k, use, n, par)
                        if (g, p) == (1, 0) and live(n - 3):
                            act.wait_ge(mean_var_done, KT * (n - 2))
                            wait(act, norm_done, KT * (n - 3))
                            nc.scalar.activation(log_var[:, :], mean_var[1 - par][:, :, 1], ACT.Ln,
                                                 bias=eps_col[:, 0:1]).then_inc(log_done, 1)
                            act.wait_ge(log_done, n - 2)
                            nc.scalar.activation(rstd[:, :], log_var[:, :], ACT.Exp, scale=-0.5).then_inc(rstd_done, 1)

            nc.scalar.preload_act_table_set("natural_log_exp_and_others")
            act.wait_ge(consts_in, 48)
            act.wait_ge(ones_set, 3)
            slots(act, slot)

        @block.vector
        def _(dve):
            bank = {(use[2], use[5]): use[4] for use in SHARED}

            def negate(n, half):
                hi, lo = neg_max[half][:, :, :, 0, :], neg_max[half][:, :, :, 1, :]
                top = row_max[:, :, :, MP * half:MP * (half + 1)]
                dve.wait_ge(max_done, H * n + H // 2 * (half + 1))
                nc.vector.tensor_scalar(hi, top, -1.0, None, ALU.mult).then_inc(neg_hi_done, 1)
                dve.wait_ge(neg_hi_done, 2 * n + half + 1)
                nc.vector.scalar_tensor_tensor(out=lo, in0=top, scalar=-1.0, in1=hi, op0=ALU.mult,
                                               op1=ALU.subtract).then_inc(neg_lo_done, 1)

            def divide(b, t, bank):
                heads = shared[bank][:, :].rearrange("p (h c) -> p h c", c=2 * DK)
                dve.wait_ge(out_turn_full, KT * b + t + 1)
                nc.vector.reciprocal(inv_sum[:, t, :], heads[:, :, DK]).then_inc(inv_done, 1)
                dve.wait_ge(inv_done, KT * b + t + 1)
                nc.vector.tensor_tensor(context[:, t, :].rearrange("p (h d) -> p h d", d=DK), heads[:, :, 0:DK],
                                        inv_sum[:, t, :].unsqueeze(2).broadcast_to([P, H, DK]),
                                        ALU.mult).then_inc(context_done, 1)

            def split_qk_lo(b, m):
                for f in range(2):
                    rows, others = slice(HALF * f, HALF * (f + 1)), slice(HALF * (1 - f), HALF * (2 - f))
                    dve.wait_ge(qk_hi_done, 4 * b + 2 * m + f + 1)
                    nc.vector.tensor_tensor(qk_parts[m][f][others, :, :], qk_raw[m][rows, :, :],
                                            qk_parts[m][f][rows, :, :], ALU.subtract).then_inc(qk_lo_done, 1)

            def slot(n, par):
                b = n - 2
                for g in range(GROUPS):
                    for p in range(2):
                        if (g, p) == (0, 1) and live(n - 3):
                            dve.wait_ge(stats_done, KT * (n - 2))
                        for side in range(2):
                            if live(n):
                                dve.wait_ge(max_full, H * n + GH * g + 2 * p + side + 1)
                                nc.vector.tensor_reduce(row_max[:, :, side, 2 * g + p], max_ps[side][:, :, :], AX.X,
                                                        ALU.max).then_inc(max_done, 1)
                        if p == 1 and g % 2 == 1 and live(n):
                            negate(n, g // 2)
                        if (g, p) == (0, 0) and live(n - 3):
                            dve.wait_ge(z_done, n - 2)
                            for t in range(KT):
                                nc.vector.bn_stats(stats[:, t, :], z[1 - par][:, t, :]).then_inc(stats_done, 1)
                        if (g, p) == (0, 1) and live(n - 3):
                            for t in range(KT):
                                nc.vector.bn_aggr(mean_var[1 - par][:, t, :], stats[:, t, :]).then_inc(mean_var_done, 1)
                        if (g, p) == (1, 0) and is_last(n - 3):
                            dve.wait_ge(rstd_done, B)
                            dve.wait_ge(stored[1 - par], 8 * (n - 3 - (1 - par)))
                            dve.wait_ge(beta_done, B - 1)
                            norm(dve, nc.vector, n - 3, 1 - par)
                        if (g, p) in ((1, 0), (2, 0)) and live(n + 1):
                            split_qk_lo(n + 1, g - 1)
                        if (g, p) == (1, 1) and live(b):
                            for t in range(KT):
                                divide(b, t, bank["out_turn", t])
                        if (g, p) == (2, 1) and live(b):
                            dve.wait_ge(context_hi_done, b + 1)
                            nc.vector.tensor_tensor(context_lo[:, :, :].rearrange("p k s -> p (k s)"),
                                                    shared[bank["ctx_turn", 0]][:, :],
                                                    context_hi[:, :, :].rearrange("p k s -> p (k s)"),
                                                    ALU.subtract).then_inc(context_lo_done, 1)
                        if (g, p) == (3, 1) and live(b):
                            dve.wait_ge(out_full, b + 1)
                            dve.wait_ge(x_bias_done, b + 1)
                            wait(dve, norm_done, KT * (b - 1))
                            nc.vector.tensor_tensor(z[par][:, :, :].rearrange("p t d -> p (t d)"),
                                                    shared[bank["out_proj", 0]][:, :],
                                                    x_in[par][:, :, :].rearrange("p t d -> p (t d)"),
                                                    ALU.add).then_inc(z_done, 1)

            def split_weights(matrices, count):
                nc.vector.tensor_copy(w_hi[:, :, matrices, :], w_raw[:, :, matrices, :]).then_inc(weights_split, 1)
                dve.wait_ge(weights_split, count + 1)
                nc.vector.tensor_tensor(w_lo[:, :, matrices, :], w_raw[:, :, matrices, :], w_hi[:, :, matrices, :],
                                        ALU.subtract).then_inc(weights_split, 1)

            def output_bias():
                dve.wait_ge(bias_prod, 1)
                nc.vector.tensor_tensor(bias_out[:, :], ctx_ps[:, 0:D], row_params[:, 0, :],
                                        ALU.add).then_inc(bias_out_done, 1)

            dve.wait_ge(weights_in, 16)
            split_weights(slice(0, 2), 0)
            dve.wait_ge(consts_in, 48)
            nc.vector.tensor_copy(sel[:, :, :, :, :], sel_raw[:, :, :, :, :]).then_inc(consts_done, 1)
            dve.wait_ge(xc_in[1], 32)
            dve.wait_ge(xc_lo_done, 2)
            for a in range(2):
                nc.vector.tensor_copy(xc_hi[1][:, a], xc_raw[1][:, a]).then_inc(xc_hi_done, 1)
                dve.wait_ge(xc_hi_done, 3 + a)
                nc.vector.tensor_tensor(xc_lo[1][:, a], xc_raw[1][:, a], xc_hi[1][:, a], ALU.subtract
                                        ).then_inc(xc_lo_done, 1)
            dve.wait_ge(weights_rest_in, 16)
            split_weights(slice(2, 4), 2)
            dve.wait_ge(rows_in, 48)
            nc.vector.tensor_copy(ident_r[:, :], ident[:, :]).then_inc(consts_done, 1)
            nc.vector.tensor_copy(bias_v_wide[:, :, :], bias_v[:, :].unsqueeze(2).broadcast_to([P, KT, P])
                                  ).then_inc(consts_done, 1)
            slots(dve, slot, output_bias)

        @block.gpsimd
        def _(pool):
            def split_xc(b, bp, a):
                if not isinstance(b, int) or b > 0:
                    wait(pool, xc_in[bp], 16 * (b - bp) + 32 - 16 * (1 - bp))
                else:
                    pool.wait_ge(xc_in[0] if a else x_first_in, 16)
                if a == 1:
                    wait(pool, v_full, b - 1)
                nc.gpsimd.tensor_tensor(xc_hi[bp][:, a], xc_raw[bp][:, a],
                                        one_col[:, :].unsqueeze(2).broadcast_to([P, KT, S]),
                                        ALU.mult).then_inc(xc_hi_done, 1)
                pool.wait_ge(xc_hi_done, 2 * b + a + 1)
                nc.gpsimd.tensor_tensor(xc_lo[bp][:, a], xc_raw[bp][:, a], xc_hi[bp][:, a],
                                        ALU.subtract).then_inc(xc_lo_done, 1)

            def split_qk_hi(b, m):
                for f in range(2):
                    if f == 0:
                        wait(pool, qk_raw_done, 2 * b + m + 1)
                    nc.gpsimd.tensor_tensor(qk_parts[m][f][:, :, :], qk_raw[m][:, :, :],
                                            one_col[:, :].unsqueeze(2).broadcast_to([P, 2, S]),
                                            ALU.mult).then_inc(qk_hi_done, 1)

            def slot(n, par):
                if live(n + 1):
                    split_qk_hi(n + 1, 0)
                    if not live(n):
                        split_qk_hi(n + 1, 1)
                if live(n - 2):
                    pool.wait_ge(x_in_loaded[par], 8 * (n - 2 - par) + 16)
                    nc.gpsimd.tensor_tensor(x_in[par][:, :, :], x_in[par][:, :, :],
                                            bias_out[:, :].unsqueeze(1).broadcast_to([P, KT, D]),
                                            ALU.add).then_inc(x_bias_done, 1)
                if live(n + 2) and live(n):
                    split_xc(n + 2, par, 0)
                if live(n - 3) and not is_last(n - 3):
                    pool.wait_ge(rstd_done, n - 2)
                    wait(pool, stored[1 - par], 8 * (n - 3 - (1 - par)))
                if live(n + 1) and live(n):
                    split_qk_hi(n + 1, 1)
                if live(n - 3) and not is_last(n - 3):
                    norm(pool, nc.gpsimd, n - 3, 1 - par)
                if live(n + 2) and live(n):
                    split_xc(n + 2, par, 1)

            for p in range(2):
                nc.gpsimd.memset(v_ones[p][:, :, :, :], 1.0).then_inc(ones_set, 1)
            nc.gpsimd.memset(eps_col[:, :], EPS).then_inc(ones_set, 1)
            nc.gpsimd.memset(one_col[:, :], 1.0).then_inc(ones_set, 1)
            pool.wait_ge(ones_set, 4)
            for a in range(2):
                split_xc(0, 0, a)
            slots(pool, slot, lambda: pool.wait_ge(bias_out_done, 1))


def kernel(x, ctx_1024, L0_xattn_W_qkv, L0_xattn_b_qkv, L0_xattn_W_o, L0_xattn_b_o, L0_xattn_ln_gamma, L0_xattn_ln_beta):
    import numpy as np
    from concourse import bacc
    from concourse.bass_utils import run_bass_kernel_spmd

    x, c = np.asarray(x), np.asarray(ctx_1024)
    w_qkv, w_o = np.asarray(L0_xattn_W_qkv), np.asarray(L0_xattn_W_o)
    b_qkv = np.asarray(L0_xattn_b_qkv)

    w = np.stack([w_qkv[:D].T, w_qkv[D:2 * D].T, w_qkv[2 * D:].T, w_o.T], axis=1)
    b_q_k = np.stack([b_qkv[a * D:(a + 1) * D][m * P:(m + 1) * P] for m in range(KT) for a in range(2)], axis=1)

    select = np.zeros((P, 2, 2, 2, P), np.float32)
    for a, (hi_places, lo_place) in enumerate((((0, 2), 1), ((0, 1), 2))):
        for f in range(2):
            for j in range(2):
                for side in range(2):
                    for d in range(DK):
                        feature = 2 * DK * j + DK * side + d
                        for place in hi_places:
                            select[HALF * f + feature, f, a, j, HALF * side + DK * place + d] = 1
                        select[HALF * (1 - f) + feature, f, a, j, HALF * side + DK * lo_place + d] = 1
    ones_rows = np.zeros((P, 1), np.float32)
    for side in range(2):
        ones_rows[HALF * side + PARTS:HALF * side + ROWS] = 1

    arrays = {
        "x_t": x.transpose(0, 2, 1), "c_t": c.transpose(0, 2, 1), "x": x, "w": w, "b_q_k": b_q_k, "b_v": b_qkv[2 * D:].reshape(KT, P).T,
        "rows": np.stack([np.asarray(L0_xattn_b_o), np.asarray(L0_xattn_ln_gamma), np.asarray(L0_xattn_ln_beta)]),
        "select": select, "ident": np.eye(P, dtype=np.float32), "ones_rows": ones_rows,
    }
    arrays = {f"in_{name}": np.ascontiguousarray(a) for name, a in arrays.items()}
    nc = bacc.Bacc("TRN2", target_bir_lowering=False, num_devices=1)
    args = [nc.dram_tensor(name, a.shape, mybir.dt.from_np(a.dtype), kind="ExternalInput").ap() for name, a in arrays.items()]
    args.append(nc.dram_tensor("out", (B, S, D), F32, kind="ExternalOutput").ap())
    xattn_kernel(nc, *args)
    return run_bass_kernel_spmd(nc, [arrays], core_ids=[0]).results[0]["out"]
```
